# Optimizing a Trainium2 kernel written in Bass

```python
import numpy as np
import jax
import jax.numpy as jnp

def _softmax(x, axis=-1):
    return jax.nn.softmax(x, axis=axis)

def _gelu(x):
    return jax.nn.gelu(x, approximate=True)

def _silu(x):
    return jax.nn.silu(x)

def _sigmoid(x):
    return jax.nn.sigmoid(x)

def _layernorm(x, axis=-1, eps=1e-05):
    m = jnp.mean(x, axis=axis, keepdims=True)
    v = jnp.var(x, axis=axis, keepdims=True)
    return (x - m) / jnp.sqrt(v + eps)

def _scatter_add(tgt, idx, src, axis=0):
    return tgt.at[idx].add(src)

def _segment_sum(src, seg, n):
    return jax.ops.segment_sum(src, seg, n)
kernel_name = 'mk_adaln_attn_ffn_d1_seqx_r4_e9f8de'

def setup_inputs(seed: int=0):
    np.random.seed(seed)
    _w = jnp.asarray

    def _rec_inputs():
        import jax
        import jax.numpy as jnp
        _rk = jax.random.key(seed)
        x = 8.748e-05 + 1 * jax.random.normal(jax.random.fold_in(_rk, 1), (4, 512, 512), jnp.float32)
        _lenS = 512 - jax.random.randint(jax.random.fold_in(_rk, 7), (4,), 0, max(1, 512 // 4) + 1, jnp.int32)
        _lenS2 = 512 - jax.random.randint(jax.random.fold_in(_rk, 8), (4,), 0, max(1, 512 // 4) + 1, jnp.int32)
        cond_2048 = -9.80646e-05 + 1.00041 * jax.random.normal(jax.random.fold_in(_rk, 11), (4, 512), jnp.float32)
        return (x, cond_2048)
    x, cond_2048 = _rec_inputs()

    def _L0_cond_setup():
        import jax, jax.numpy as jnp
        import numpy as np
        DT = 0.01
        EPSILON = 0.08
        ALPHA = 0.7
        BETA = 0.8
        CLAMP = 20.0
        B, T, N = (64, 128, 512)

        def _derivative(q, p, drive, coupling, bias):
            i_couple = jnp.tanh(q) @ coupling.T
            dq = q - q ** 3 / 3.0 - p + drive + i_couple + bias
            dp = EPSILON * (q + ALPHA - BETA * p)
            return (dq, dp)

        def _rk4_step(q, p, drive, coupling, bias):
            dq1, dp1 = _derivative(q, p, drive, coupling, bias)
            dq2, dp2 = _derivative(q + 0.5 * DT * dq1, p + 0.5 * DT * dp1, drive, coupling, bias)
            dq3, dp3 = _derivative(q + 0.5 * DT * dq2, p + 0.5 * DT * dp2, drive, coupling, bias)
            dq4, dp4 = _derivative(q + DT * dq3, p + DT * dp3, drive, coupling, bias)
            q_next = q + DT / 6.0 * (dq1 + 2 * dq2 + 2 * dq3 + dq4)
            p_next = p + DT / 6.0 * (dp1 + 2 * dp2 + 2 * dp3 + dp4)
            q_next = jnp.clip(q_next, -CLAMP, CLAMP)
            p_next = jnp.clip(p_next, -CLAMP, CLAMP)
            return (q_next, p_next)
        key = jax.random.key(seed)
        k1, k2, k3, k4 = jax.random.split(key, 4)
        return {'q0': jax.random.normal(k1, (B, N), dtype=jnp.float32), 'p0': jax.random.normal(k2, (B, N), dtype=jnp.float32), 'input_drive_seq': jax.random.normal(k3, (B, T, N), dtype=jnp.float32), 'coupling': jax.random.normal(k4, (N, N), dtype=jnp.float32) * 0.01, 'bias': jnp.zeros((N,), dtype=jnp.float32)}
    _L0_cond_all = _L0_cond_setup()
    _L0_cond_in = {k: v for k, v in _L0_cond_all.items() if k in ('coupling', 'bias')}
    del _L0_cond_all

    def _L0_attn_setup():
        import jax, jax.numpy as jnp
        import numpy as np
        HIDDEN = 512
        N_HEADS = 16
        HEAD_DIM = HIDDEN // N_HEADS
        ROTARY_DIM = 32
        ROPE_BASE = 10000.0
        NEG_INF = -10000.0

        def _rope_cos_sin(seqlen, dtype):
            inv_freq = 1.0 / ROPE_BASE ** (jnp.arange(0, ROTARY_DIM, 2, dtype=jnp.float32) / ROTARY_DIM)
            t = jnp.arange(seqlen, dtype=jnp.float32)
            freqs = jnp.outer(t, inv_freq)
            return (jnp.cos(freqs).astype(dtype), jnp.sin(freqs).astype(dtype))

        def _apply_rotary(u, cos, sin):
            u_rot, u_pass = (u[..., :ROTARY_DIM], u[..., ROTARY_DIM:])
            u1, u2 = (u_rot[..., :ROTARY_DIM // 2], u_rot[..., ROTARY_DIM // 2:])
            c = cos[None, :, None, :]
            s = sin[None, :, None, :]
            rot = jnp.concatenate([u1 * c - u2 * s, u1 * s + u2 * c], axis=-1)
            return jnp.concatenate([rot, u_pass], axis=-1)
        key = jax.random.key(seed)
        k1, k2, k3 = jax.random.split(key, 3)
        x = jax.random.normal(k1, (2, 512, HIDDEN), dtype=jnp.float32)
        Wqkv_w = jax.random.normal(k2, (3 * HIDDEN, HIDDEN), dtype=jnp.float32) * (1.0 / np.sqrt(HIDDEN))
        Wqkv_b = jax.random.normal(k3, (3 * HIDDEN,), dtype=jnp.float32) * 0.01
        return {'x': x, 'Wqkv_w': Wqkv_w, 'Wqkv_b': Wqkv_b}
    _L0_attn_all = _L0_attn_setup()
    _L0_attn_in = {k: v for k, v in _L0_attn_all.items() if k in ('Wqkv_w', 'Wqkv_b')}
    del _L0_attn_all

    def _L0_cond2_setup():
        import jax, jax.numpy as jnp
        import numpy as np
        DIM = 512
        H = 16
        DH = 128
        INNER = H * DH
        MLP = 4 * DIM
        B, T = (2, 512)
        EPS = 1e-06

        def _ln(x):
            mu = jnp.mean(x, axis=-1, keepdims=True)
            var = jnp.var(x, axis=-1, keepdims=True)
            return (x - mu) * jax.lax.rsqrt(var + EPS)
        key = jax.random.key(seed)
        ks = jax.random.split(key, 12)
        s = 0.02
        return {'x': jax.random.normal(ks[0], (B, T, DIM), jnp.float32), 'timestep_embed': jax.random.normal(ks[1], (B, DIM), jnp.float32), 'ada_w': jax.random.normal(ks[2], (DIM, 6 * DIM), jnp.float32) * s, 'ada_b': jnp.zeros((6 * DIM,), jnp.float32), 'qkv_w': jax.random.normal(ks[3], (DIM, 3 * INNER), jnp.float32) * s, 'qkv_b': jnp.zeros((3 * INNER,), jnp.float32), 'out_w': jax.random.normal(ks[4], (INNER, DIM), jnp.float32) * s, 'out_b': jnp.zeros((DIM,), jnp.float32), 'ffn_w1': jax.random.normal(ks[5], (DIM, MLP), jnp.float32) * s, 'ffn_b1': jnp.zeros((MLP,), jnp.float32), 'ffn_w2': jax.random.normal(ks[6], (MLP, DIM), jnp.float32) * s, 'ffn_b2': jnp.zeros((DIM,), jnp.float32)}
    _L0_cond2_all = _L0_cond2_setup()
    _L0_cond2_in = {k: v for k, v in _L0_cond2_all.items() if k in ('ada_w', 'ada_b', 'qkv_w', 'qkv_b', 'out_w', 'out_b', 'ffn_w1', 'ffn_b1', 'ffn_w2', 'ffn_b2')}
    del _L0_cond2_all

    def _L0_ffn_setup():
        import jax, jax.numpy as jnp
        import numpy as np

        @jax.custom_vjp
        def ste_sign(x):
            return jnp.sign(x)

        def _ste_fwd(x):
            return (jnp.sign(x), None)

        def _ste_bwd(_, g):
            return (g,)
        ste_sign.defvjp(_ste_fwd, _ste_bwd)
        D_MODEL = 512
        D_HIDDEN = 2048
        key = jax.random.key(seed)
        k_x, k_up, k_dn = jax.random.split(key, 3)
        x = jax.random.normal(k_x, (2, 512, D_MODEL), dtype=jnp.float32)
        up_weight = jax.random.normal(k_up, (D_HIDDEN, D_MODEL), dtype=jnp.float32) * 0.02
        down_weight = jax.random.normal(k_dn, (D_MODEL, D_HIDDEN), dtype=jnp.float32) * 0.02
        up_scale = jnp.ones((D_HIDDEN,), dtype=jnp.float32)
        down_scale = jnp.ones((D_MODEL,), dtype=jnp.float32)
        output_scale = jnp.ones((1,), dtype=jnp.float32)
        return {'x': x, 'up_weight': up_weight, 'down_weight': down_weight, 'up_scale': up_scale, 'down_scale': down_scale, 'output_scale': output_scale}
    _L0_ffn_all = _L0_ffn_setup()
    _L0_ffn_in = {k: v for k, v in _L0_ffn_all.items() if k in ('up_weight', 'down_weight', 'up_scale', 'down_scale', 'output_scale')}
    del _L0_ffn_all
    return {'x': x, 'cond_2048': cond_2048, 'L0_cond_coupling': _L0_cond_in['coupling'], 'L0_cond_bias': _L0_cond_in['bias'], 'L0_attn_Wqkv_w': _L0_attn_in['Wqkv_w'], 'L0_attn_Wqkv_b': _L0_attn_in['Wqkv_b'], 'L0_cond2_ada_w': _L0_cond2_in['ada_w'], 'L0_cond2_ada_b': _L0_cond2_in['ada_b'], 'L0_cond2_qkv_w': _L0_cond2_in['qkv_w'], 'L0_cond2_qkv_b': _L0_cond2_in['qkv_b'], 'L0_cond2_out_w': _L0_cond2_in['out_w'], 'L0_cond2_out_b': _L0_cond2_in['out_b'], 'L0_cond2_ffn_w1': _L0_cond2_in['ffn_w1'], 'L0_cond2_ffn_b1': _L0_cond2_in['ffn_b1'], 'L0_cond2_ffn_w2': _L0_cond2_in['ffn_w2'], 'L0_cond2_ffn_b2': _L0_cond2_in['ffn_b2'], 'L0_ffn_up_weight': _L0_ffn_in['up_weight'], 'L0_ffn_down_weight': _L0_ffn_in['down_weight'], 'L0_ffn_up_scale': _L0_ffn_in['up_scale'], 'L0_ffn_down_scale': _L0_ffn_in['down_scale'], 'L0_ffn_output_scale': _L0_ffn_in['output_scale']}

def reference(x, cond_2048, L0_cond_coupling, L0_cond_bias, L0_attn_Wqkv_w, L0_attn_Wqkv_b, L0_cond2_ada_w, L0_cond2_ada_b, L0_cond2_qkv_w, L0_cond2_qkv_b, L0_cond2_out_w, L0_cond2_out_b, L0_cond2_ffn_w1, L0_cond2_ffn_b1, L0_cond2_ffn_w2, L0_cond2_ffn_b2, L0_ffn_up_weight, L0_ffn_down_weight, L0_ffn_up_scale, L0_ffn_down_scale, L0_ffn_output_scale):
    import jax
    import jax.numpy as jnp

    def _L0_cond_ref(q0, p0, input_drive_seq, coupling, bias):
        import jax, jax.numpy as jnp
        import numpy as np
        DT = 0.01
        EPSILON = 0.08
        ALPHA = 0.7
        BETA = 0.8
        CLAMP = 20.0
        B, T, N = (64, 128, 512)

        def _derivative(q, p, drive, coupling, bias):
            i_couple = jnp.tanh(q) @ coupling.T
            dq = q - q ** 3 / 3.0 - p + drive + i_couple + bias
            dp = EPSILON * (q + ALPHA - BETA * p)
            return (dq, dp)

        def _rk4_step(q, p, drive, coupling, bias):
            dq1, dp1 = _derivative(q, p, drive, coupling, bias)
            dq2, dp2 = _derivative(q + 0.5 * DT * dq1, p + 0.5 * DT * dp1, drive, coupling, bias)
            dq3, dp3 = _derivative(q + 0.5 * DT * dq2, p + 0.5 * DT * dp2, drive, coupling, bias)
            dq4, dp4 = _derivative(q + DT * dq3, p + DT * dp3, drive, coupling, bias)
            q_next = q + DT / 6.0 * (dq1 + 2 * dq2 + 2 * dq3 + dq4)
            p_next = p + DT / 6.0 * (dp1 + 2 * dp2 + 2 * dp3 + dp4)
            q_next = jnp.clip(q_next, -CLAMP, CLAMP)
            p_next = jnp.clip(p_next, -CLAMP, CLAMP)
            return (q_next, p_next)
        drive_tbn = jnp.swapaxes(input_drive_seq, 0, 1)

        def scan_fn(carry, drive):
            q, p = carry
            q, p = _rk4_step(q, p, drive, coupling, bias)
            return ((q, p), q)
        (_, _), q_trace_tbn = jax.lax.scan(scan_fn, (q0, p0), drive_tbn)
        return jnp.swapaxes(q_trace_tbn, 0, 1)

    def _L0_attn_ref(x, Wqkv_w, Wqkv_b):
        import jax, jax.numpy as jnp
        import numpy as np
        HIDDEN = 512
        N_HEADS = 16
        HEAD_DIM = HIDDEN // N_HEADS
        ROTARY_DIM = 32
        ROPE_BASE = 10000.0
        NEG_INF = -10000.0

        def _rope_cos_sin(seqlen, dtype):
            inv_freq = 1.0 / ROPE_BASE ** (jnp.arange(0, ROTARY_DIM, 2, dtype=jnp.float32) / ROTARY_DIM)
            t = jnp.arange(seqlen, dtype=jnp.float32)
            freqs = jnp.outer(t, inv_freq)
            return (jnp.cos(freqs).astype(dtype), jnp.sin(freqs).astype(dtype))

        def _apply_rotary(u, cos, sin):
            u_rot, u_pass = (u[..., :ROTARY_DIM], u[..., ROTARY_DIM:])
            u1, u2 = (u_rot[..., :ROTARY_DIM // 2], u_rot[..., ROTARY_DIM // 2:])
            c = cos[None, :, None, :]
            s = sin[None, :, None, :]
            rot = jnp.concatenate([u1 * c - u2 * s, u1 * s + u2 * c], axis=-1)
            return jnp.concatenate([rot, u_pass], axis=-1)
        B, S, _ = x.shape
        qkv = jnp.einsum('bse,oe->bso', x, Wqkv_w) + Wqkv_b
        qkv = qkv.reshape(B, S, 3, N_HEADS, HEAD_DIM)
        cos, sin = _rope_cos_sin(S, x.dtype)
        q = _apply_rotary(qkv[:, :, 0], cos, sin)
        k = _apply_rotary(qkv[:, :, 1], cos, sin)
        v = qkv[:, :, 2]
        scale = 1.0 / np.sqrt(HEAD_DIM)
        scores = jnp.einsum('bthd,bshd->bhts', q, k * scale)
        causal_mask = jnp.triu(jnp.full((S, S), NEG_INF, dtype=scores.dtype), 1)
        scores = scores + causal_mask
        attn = jax.nn.softmax(scores, axis=-1)
        out = jnp.einsum('bhts,bshd->bthd', attn, v)
        return out.reshape(B, S, N_HEADS * HEAD_DIM)

    def _L0_cond2_ref(x, timestep_embed, ada_w, ada_b, qkv_w, qkv_b, out_w, out_b, ffn_w1, ffn_b1, ffn_w2, ffn_b2):
        import jax, jax.numpy as jnp
        import numpy as np
        DIM = 512
        H = 16
        DH = 128
        INNER = H * DH
        MLP = 4 * DIM
        B, T = (2, 512)
        EPS = 1e-06

        def _ln(x):
            mu = jnp.mean(x, axis=-1, keepdims=True)
            var = jnp.var(x, axis=-1, keepdims=True)
            return (x - mu) * jax.lax.rsqrt(var + EPS)
        Bc, Tc, D = x.shape
        ada = (timestep_embed @ ada_w + ada_b)[:, None, :]
        shift1, scale1, gate1, shift2, scale2, gate2 = jnp.split(ada, 6, axis=-1)
        x1 = _ln(x) * (1.0 + scale1) + shift1
        qkv = (x1 @ qkv_w + qkv_b).reshape(Bc, Tc, 3, H, DH)
        q, k, v = (qkv[:, :, 0], qkv[:, :, 1], qkv[:, :, 2])
        scale = DH ** (-0.5)
        attn = jnp.einsum('bthd,bshd->bhts', q, k) * scale
        attn = jax.nn.softmax(attn, axis=-1)
        attn_out = jnp.einsum('bhts,bshd->bthd', attn, v).reshape(Bc, Tc, INNER)
        attn_out = attn_out @ out_w + out_b
        x = x + gate1 * attn_out
        x2 = _ln(x) * (1.0 + scale2) + shift2
        h = jax.nn.gelu(x2 @ ffn_w1 + ffn_b1, approximate=False)
        x = x + gate2 * (h @ ffn_w2 + ffn_b2)
        return x

    def _L0_ffn_ref(x, up_weight, down_weight, up_scale, down_scale, output_scale):
        import jax, jax.numpy as jnp
        import numpy as np

        @jax.custom_vjp
        def ste_sign(x):
            return jnp.sign(x)

        def _ste_fwd(x):
            return (jnp.sign(x), None)

        def _ste_bwd(_, g):
            return (g,)
        ste_sign.defvjp(_ste_fwd, _ste_bwd)
        D_MODEL = 512
        D_HIDDEN = 2048
        up_w = ste_sign(up_weight)
        down_w = ste_sign(down_weight)
        hidden = jnp.einsum('bsd,hd->bsh', x, up_w) * up_scale
        hidden = jax.nn.relu(hidden)
        out = jnp.einsum('bsh,dh->bsd', hidden, down_w) * down_scale
        return out * output_scale
    x = x + _L0_attn_ref(_L0_cond_ref(cond_2048, cond_2048, x, L0_cond_coupling, L0_cond_bias), L0_attn_Wqkv_w, L0_attn_Wqkv_b)
    x = x + _L0_ffn_ref(_L0_cond2_ref(x, cond_2048, L0_cond2_ada_w, L0_cond2_ada_b, L0_cond2_qkv_w, L0_cond2_qkv_b, L0_cond2_out_w, L0_cond2_out_b, L0_cond2_ffn_w1, L0_cond2_ffn_b1, L0_cond2_ffn_w2, L0_cond2_ffn_b2), L0_ffn_up_weight, L0_ffn_down_weight, L0_ffn_up_scale, L0_ffn_down_scale, L0_ffn_output_scale)
    return x

_drawn_inputs = setup_inputs


def setup_inputs(seed=0):
    import zlib

    import numpy as np

    out = dict(_drawn_inputs(seed))
    spreads = {'L0_cond_bias': (0.0, 0.1),
     'L0_cond2_ada_b': (0.0, 0.1),
     'L0_cond2_qkv_b': (0.0, 0.29),
     'L0_cond2_out_b': (0.0, 0.1),
     'L0_cond2_ffn_b1': (0.0, 0.494),
     'L0_cond2_ffn_b2': (0.0, 0.1),
     'L0_ffn_up_scale': (1.0, 0.2),
     'L0_ffn_down_scale': (1.0, 0.2)}
    factors = {'L0_attn_Wqkv_b': 7.643}
    for name, (base, spread) in spreads.items():
        noise = np.random.default_rng([zlib.crc32(name.encode()), seed]).standard_normal(out[name].shape)
        drawn = base * np.exp(spread * noise) if base else spread * noise
        out[name] = jnp.asarray(drawn.astype(out[name].dtype))
    for name, factor in factors.items():
        out[name] = (out[name] * factor).astype(out[name].dtype)
    return out
```

```python
from contextlib import ExitStack

import numpy as np
import concourse.bass as bass
from concourse import mybir

F32 = mybir.dt.float32
F32R = mybir.dt.float32r
F16 = mybir.dt.float16
ALU = mybir.AluOpType
ACT = mybir.ActivationFunctionType
AX = mybir.AxisListType

P = 128
B, T, D = 4, 512, 512
C = D // P
TOK = B * T
TT = T // P

DT, EPSILON, ALPHA, BETA, CLAMP = 0.01, 0.08, 0.7, 0.8, 20.0
W_SCALE = 64.0
STAGES = 4
START_OF = [0, 0, 1, 2]
POOL_STEP = 16
STAGE_STEP = [DT / 2, DT / 2, DT, DT / 6]


class Count:

    def __init__(self, sem, start=0):
        self.sem, self.now = sem, start

    def inc(self, ins, by=1):
        ins.then_inc(self.sem, by)
        self.now += by
        return self.now


def scan_phase(nc, io, x_dram, trace_dram, cond_dram):
    sems = []
    with ExitStack() as ctx:
        def sb(n, s, d): return ctx.enter_context(nc.sbuf_tensor(n, s, d))
        def ps(n): return ctx.enter_context(nc.psum_tensor(n, [P, 512], F32))
        def sem(n):
            sems.append(nc.alloc_semaphore(n))
            return sems[-1]
        xT = sb("xT", [P, C, B, T], F32)
        condT = sb("condT", [P, C, B], F32)
        identity = sb("identity", [P, P], F32)
        rows = sb("rows", [P, 4, D], F32)
        coup = sb("coup", [P, C, D], F32)
        cond_rows = sb("cond_rows", [B, D], F32)
        wT = sb("wT", [P, C, D], F32)
        w_hi = sb("w_hi", [P, C, D], F16)
        w_lo = sb("w_lo", [P, C, D], F16)
        bias_c = sb("bias_c", [P, C], F32)
        bias = sb("bias", [P, C, B], F32)
        trace = sb("trace", [P, C, B, T + 1], F32)
        tanh_parts = sb("tanh_parts", [P, 2, C, 2, B], F16)
        tanh_full = sb("tanh_full", [P, 2, C, B], F32)
        scratch = sb("scratch", [P, 8], F32)
        q_new = sb("q_new", [P, C, B], F32)
        q = sb("q", [P, STAGES, C, B], F32)
        pst = sb("pst", [P, STAGES, C, B], F32)
        p_new = sb("p_new", [P, C, B], F32)
        drive = sb("drive", [P, C, B], F32)
        rate = sb("rate", [P, STAGES, C, B], F32)
        z_sum = sb("z_sum", [P, C, B], F32)
        pz_sum = sb("pz_sum", [P, C, B], F32)
        start_p = sb("start_p", [P, STAGES, C, B], F32)
        start_q = sb("start_q", [P, C, B], F32)
        start = sb("start", [P, 3, C, B], F32)
        p_alpha = sb("p_alpha", [P, 2, C, B], F32)
        cub = sb("cub", [P, C, B], F32)
        slope = sb("slope", [P, C, B], F32)
        local = sb("local", [P, C, B], F32)
        base = sb("base", [P, C, B], F32)
        base_lo = sb("base_lo", [P, C, B], F32)
        gp = sb("gp", [P, 11, C, B], F32)
        consts = sb("consts", [P, 10, C, B], F32)
        banks = [ps(f"bank{i}") for i in range(4)]
        s_rows = [sem(f"s_rows{i}") for i in range(2)]
        s_coup, s_small, s_tr, s_ev, s_w, s_pre = [sem("s_" + n) for n in ("coup", "small", "tr", "ev", "w", "pre")]
        s_q = sem("s_q")
        s_clip = sem("s_clip")
        s_th = sem("s_th")
        s_tf = sem("s_tf")
        s_tl = sem("s_tl")
        s_mm = sem("s_mm")
        s_rate = sem("s_rate")
        s_start = sem("s_start")
        s_drive = sem("s_drive")
        s_z = sem("s_z")
        s_pz = sem("s_pz")
        s_palpha = sem("s_palpha")
        s_pclip = sem("s_pclip")
        s_dve, s_pool = sem("s_dve"), sem("s_pool")
        s_trace = sem("s_trace")
        s_table, s_out = sem("s_table"), sem("s_out")
        block = ctx.enter_context(nc.Block())

        x_tiles = io["x"].rearrange("b (i r p) d -> (b i) p r d", p=P, r=2)
        PAIRS = B * TT // 2

        @block.sync
        def _(sp):
            sp.dma_start(coup[:, :, :], io["L0_cond_coupling"].rearrange("(c p) k -> p c k", p=P)).then_inc(s_coup, 16)
            for j in range(PAIRS):
                if j >= 2:
                    sp.wait_ge(s_tr, C + 2 * (j - 1))
                sp.dma_start(rows[:, 2 * (j % 2):2 * (j % 2) + 2, :], x_tiles[j]).then_inc(s_rows[j % 2], 16)
            sp.wait_ge(s_ev, C + 2 * PAIRS)
            sp.dma_start(x_dram, xT[:, :, :, :]).then_inc(s_out, 16)
            sp.wait_ge(s_w, 3)
            sp.dma_start(cond_dram, condT[:, :, :]).then_inc(s_out, 16)
            sp.wait_ge(s_trace, 1)
            sp.dma_start(trace_dram, trace[:, :, :, 1:T + 1]).then_inc(s_out, 16)
            sp.wait_ge(s_out, 48)

        @block.scalar
        def _(act):
            act.dma_start(identity[:, :], io["const_identity"]).then_inc(s_small, 16)
            act.dma_start(cond_rows[:, :], io["cond_2048"]).then_inc(s_small, 16)
            with nc.allow_non_contiguous_dma(reason="512 bias values, once"):
                act.dma_start(bias_c[:, :], io["L0_cond_bias"].rearrange("(c p) -> p c", p=P)).then_inc(s_small, 16)
            act.wait_ge(s_pre, 1)
            act.activation(scratch[:, 4:8], scratch[:, 0:4], ACT.Tanh).then_inc(s_table, 1)
            with act.Fori(0, T) as t:
                for s in range(STAGES):
                    u = s % 2
                    src = q_new[:, :, :] if s == 0 else q[:, s]
                    act.wait_ge(s_q, t * STAGES + (s + 1))
                    act.activation(tanh_parts[:, u, :, 0, :], src, ACT.Tanh).then_inc(s_th, 1)
                    act.activation(tanh_full[:, u], src, ACT.Tanh).then_inc(s_tf, 1)

        @block.tensor
        def _(pe):
            pe.wait_ge(s_small, 48)
            pe.wait_ge(s_coup, 16)
            for k in range(C):
                for m in range(C):
                    last = pe.matmul(banks[k][:, m * P:(m + 1) * P], coup[:, m, k * P:(k + 1) * P], identity[:, :],
                                     start=(m == 0), stop=(m == C - 1), skip_group_check=True)
                last.then_inc(s_tr, 1)
            for j in range(2 * PAIRS):
                if j % 2 == 0:
                    pe.wait_ge(s_rows[(j // 2) % 2], 16 * (j // 4 + 1))
                pe.wait_ge(s_ev, j + 1)
                for c in range(C):
                    last = pe.matmul(banks[j % 4][:, c * P:(c + 1) * P], rows[:, j % 4, c * P:(c + 1) * P], identity[:, :],
                                     start=(c == 0), stop=(c == C - 1), skip_group_check=True)
                last.then_inc(s_tr, 1)
            pe.wait_ge(s_ev, 2 * PAIRS + 1)
            for c in range(C):
                last = pe.matmul(banks[0][:, c * B:(c + 1) * B], cond_rows[:, c * P:(c + 1) * P], identity[0:B, 0:B],
                                 start=(c == 0), stop=(c == C - 1), skip_group_check=True)
            last.then_inc(s_tr, 1)
            pe.wait_ge(s_w, 3)
            with pe.Fori(0, T) as t:
                for s in range(STAGES):
                    u = s % 2
                    out = banks[u]
                    pe.wait_ge(s_th, t * STAGES + (s + 1))
                    for m in range(C):
                        for k in range(C):
                            pe.matmul(out[:, m * 8:m * 8 + 4], w_lo[:, k, m * P:(m + 1) * P], tanh_parts[:, u, k, 0, :],
                                      start=(m == 0 and k == 0), stop=False, skip_group_check=True)
                    pe.wait_ge(s_tl, t * STAGES + (s + 1))
                    for m in range(C):
                        for k in range(C):
                            last = pe.matmul(out[:, m * 8:m * 8 + 8], w_hi[:, k, m * P:(m + 1) * P], tanh_parts[:, u, k, :, :],
                                             start=False, stop=(m == C - 1 and k == C - 1), skip_group_check=True)
                    last.then_inc(s_mm, 1)

        @block.vector
        def _(v):
            v.memset(scratch[:, 0:4], 0.0).then_inc(s_pre, 1)
            for k in range(C):
                v.wait_ge(s_tr, k + 1)
                v.tensor_scalar(wT[:, k, :], banks[k][:, :], W_SCALE, None, ALU.mult).then_inc(s_ev, 1)
            v.wait_ge(s_ev, C)
            v.tensor_copy(w_hi[:, :, :], wT[:, :, :]).then_inc(s_w, 1)
            v.wait_ge(s_w, 1)
            v.tensor_tensor(w_lo[:, :, :], wT[:, :, :], w_hi[:, :, :], ALU.subtract).then_inc(s_w, 1)
            for j in range(2 * PAIRS):
                b, i = j // TT, j % TT
                v.wait_ge(s_tr, C + j + 1)
                v.tensor_copy(xT[:, :, b, i * P:(i + 1) * P], banks[j % 4][:, :].rearrange("p (c t) -> p c t", c=C)).then_inc(s_ev, 1)
            v.wait_ge(s_tr, C + 2 * PAIRS + 1)
            condv = banks[0][:, 0:C * B].rearrange("p (c b) -> p c b", c=C)
            v.tensor_copy(condT[:, :, :], condv).then_inc(s_w, 1)
            v.tensor_copy(pst[:, 0], condv).then_inc(s_pclip, 1)
            v.tensor_copy(q[:, 0], condv).then_inc(s_clip, 1)
            v.tensor_copy(q_new[:, :, :], condv).then_inc(s_q, 1)
            v.wait_ge(s_q, 1)
            with v.Fori(0, T) as t:
                n = 0

                def own(ins):
                    nonlocal n
                    ins.then_inc(s_dve, 1)
                    n += 1
                    return n

                def stt(out, in0, scalar, in1, op0=ALU.mult, op1=ALU.add):
                    return v.scalar_tensor_tensor(out=out, in0=in0, scalar=scalar, in1=in1, op0=op0, op1=op1)

                def after(mark):
                    v.wait_ge(s_dve, mark)

                v.sem_clear(s_dve)
                for s in range(STAGES):
                    u = s % 2
                    a = STAGE_STEP[s]
                    if s == 0:
                        v.wait_ge(s_clip, t + 1)
                    else:
                        v.wait_ge(s_q, t * STAGES + (s + 1))
                    cubed = own(stt(cub[:, :, :], q[:, s], -1.0 / 3.0, q[:, s], ALU.mult, ALU.mult))
                    if s == 0:
                        v.wait_ge(s_pclip, t + 1)
                    stt(rate[:, s], pst[:, s], -BETA, q[:, s]).then_inc(s_rate, 1)
                    if s == 0:
                        v.wait_ge(s_drive, t + 1)
                        begun = own(stt(start[:, 0], drive[:, :, :], DT / 2, q[:, 0]))
                    after(cubed)
                    sloped = own(stt(slope[:, :, :], cub[:, :, :], 1.0, q[:, s], ALU.add, ALU.mult))
                    if s == 0:
                        after(begun)
                        shifted = own(stt(start_p[:, 0], pst[:, 0], -DT / 2, start[:, 0]))
                    v.wait_ge(s_tf, t * STAGES + (s + 1))
                    v.tensor_tensor(tanh_parts[:, u, :, 1, :], tanh_full[:, u], tanh_parts[:, u, :, 0, :], ALU.subtract).then_inc(s_tl, 1)
                    if s == 0:
                        own(stt(start[:, 1], drive[:, :, :], DT, q[:, 0]))
                        stt(start[:, 2], drive[:, :, :], DT / 6, q[:, 0]).then_inc(s_start, 1)
                        v.wait_ge(s_palpha, t + 1)
                    if s < 3:
                        v.wait_ge(s_rate, t * STAGES + (s + 1))
                        moved = own(stt(pst[:, s + 1], rate[:, s], EPSILON * a, p_alpha[:, START_OF[s]]))
                    else:
                        v.wait_ge(s_z, t + 1)
                        shifted = own(stt(start_p[:, 3], pst[:, 3], -DT / 6, z_sum[:, :, :]))
                        after(sloped)
                        v.wait_ge(s_pz, t + 1)
                        moved = own(stt(p_new[:, :, :], rate[:, 3], EPSILON * DT / 6, pz_sum[:, :, :]))
                        after(shifted)
                        shifted = own(stt(start_q[:, :, :], q[:, 3], 1.0 / 3.0, start_p[:, 3]))
                    after(max(shifted, sloped) if s in (0, 3) else sloped)
                    based = own(stt(base[:, :, :], slope[:, :, :], a, start_q[:, :, :] if s == 3 else start_p[:, s]))
                    if s < 2:
                        after(moved)
                        shifted = own(stt(start_p[:, s + 1], pst[:, s + 1], -STAGE_STEP[s + 1], start[:, START_OF[s + 1]]))
                    if s == 3:
                        after(moved)
                        v.tensor_scalar(pst[:, 0], p_new[:, :, :], -CLAMP, CLAMP, ALU.max, ALU.min).then_inc(s_pclip, 1)
                    v.wait_ge(s_mm, t * STAGES + (s + 1))
                    after(based)
                    ov = banks[u][:, 0:C * 2 * B].rearrange("p (c h b) -> p c h b", c=C, h=2)
                    low = own(stt(base_lo[:, :, :], ov[:, :, 1, :], a / W_SCALE, base[:, :, :]))
                    dst = q[:, s + 1] if s < 3 else q_new[:, :, :]
                    after(low)
                    stt(dst, ov[:, :, 0, :], a / W_SCALE, base_lo[:, :, :]).then_inc(s_q, 1)
                v.wait_ge(s_q, t * STAGES + (STAGES + 1))
                v.tensor_scalar(q[:, 0], q_new[:, :, :], -CLAMP, CLAMP, ALU.max, ALU.min).then_inc(s_clip, 1)

        @block.gpsimd
        def _(g):
            g.wait_ge(s_small, 48)
            for b in range(B):
                last = g.tensor_copy(bias[:, :, b], bias_c[:, :])
            values = [1.0 / 3.0, EPSILON * DT / 6.0, 6 * ALPHA] + [EPSILON * ALPHA * a for a in (DT / 2, DT)]
            c_third, c_psum, c_6alpha, c_ahalf, c_afull = [consts[:, i] for i in range(len(values))]
            for i, value in enumerate(values):
                last = g.memset(consts[:, i], value)
            last.then_inc(s_pool, 1)
            g.wait_ge(s_ev, C + 2 * PAIRS)
            g.wait_ge(s_pool, 1)
            with g.Fori(0, T) as t:
                n = 0

                def own(ins):
                    nonlocal n
                    ins.then_inc(s_pool, 1)
                    n += 1
                    return n

                def tt(out, a, b, op=ALU.add):
                    return g.tensor_tensor(out, a, b, op)

                def after(mark):
                    g.wait_ge(s_pool, mark)

                g.sem_clear(s_pool)
                tt(drive[:, :, :], xT[:, :, :, bass.ds(t, 1)].rearrange("p c b o -> p c (b o)"), bias[:, :, :]).then_inc(s_drive, 1)
                g.wait_ge(s_pclip, t + 1)
                tt(p_alpha[:, 0], pst[:, 0], c_ahalf)
                tt(p_alpha[:, 1], pst[:, 0], c_afull).then_inc(s_palpha, 1)
                g.wait_ge(s_clip, t + 1)
                g.tensor_copy(trace[:, :, :, bass.ds(t, 1)].rearrange("p c b o -> p c (b o)"), q[:, 0])
                g.wait_ge(s_rate, t * STAGES + 1)
                r0 = own(tt(gp[:, 0], rate[:, 0], c_6alpha))
                g.wait_ge(s_q, t * STAGES + 2)
                d1 = own(tt(gp[:, 1], q[:, 1], q[:, 0], ALU.subtract))
                after(d1)
                m1 = own(tt(gp[:, 2], gp[:, 1], q[:, 0], ALU.subtract))
                g.wait_ge(s_q, t * STAGES + 3)
                d2 = own(tt(gp[:, 3], q[:, 2], q[:, 0], ALU.subtract))
                g.wait_ge(s_rate, t * STAGES + 3)
                r12 = own(tt(gp[:, 4], rate[:, 1], rate[:, 2]))
                after(d2)
                z1 = own(tt(gp[:, 5], gp[:, 2], gp[:, 3]))
                after(r12)
                p1 = own(tt(gp[:, 6], gp[:, 4], gp[:, 4]))
                after(z1)
                z2 = own(tt(gp[:, 7], gp[:, 5], gp[:, 3]))
                after(p1)
                p2 = own(tt(gp[:, 8], gp[:, 6], gp[:, 0]))
                after(z2)
                z3 = own(tt(gp[:, 9], gp[:, 7], c_third, ALU.mult))
                after(p2)
                p3 = own(tt(gp[:, 10], gp[:, 8], c_psum, ALU.mult))
                g.wait_ge(s_start, t + 1)
                after(z3)
                tt(z_sum[:, :, :], gp[:, 9], start[:, 2]).then_inc(s_z, 1)
                after(p3)
                tt(pz_sum[:, :, :], gp[:, 10], pst[:, 0]).then_inc(s_pz, 1)
            g.wait_ge(s_clip, T + 1)
            g.tensor_copy(trace[:, :, :, T], q[:, 0]).then_inc(s_trace, 1)
    nc.clear_and_free_semaphores(sems)
    nc.all_engine_barrier()



class Attention:

    def __init__(self, nc, ctx, heads, scale, masked):
        def sb(n, s, d): return ctx.enter_context(nc.sbuf_tensor(n, s, d))
        def ps(n): return ctx.enter_context(nc.psum_tensor(n, [P, 512], F32))
        def sem(n): return ctx.enter_context(nc.semaphore(n))
        name = "m" if masked else "f"
        self.heads, self.scale, self.masked = heads, scale, masked
        self.probs = sb(name + "_probs", [P, 2, TT, T], F32)
        self.pt = [sb(name + f"_pt_{part}", [P, TT, TT, P], F32R) for part in ("hi", "lo")]
        self.diag = sb(name + "_diag", [P, TT, P], F32)
        self.peak = sb(name + "_peak", [P, TT], F32)
        self.shift = sb(name + "_shift", [P, TT], F32)
        self.sums = sb(name + "_sums", [P, TT], F32)
        self.inverse = sb(name + "_inverse", [P, TT], F32)
        self.s_bank = [ps(name + f"_scores{i}") for i in range(2)]
        self.t_bank = [ps(name + f"_turned{i}") for i in range(2)]
        self.o_bank = ps(name + "_out")
        self.scored = sem(name + "_scored")
        self.peaked = sem(name + "_peaked")
        self.exped = sem(name + "_exped")
        self.scaled = sem(name + "_scaled")
        self.turned = sem(name + "_turned")
        self.high = sem(name + "_high")
        self.low = sem(name + "_low")
        self.valued = sem(name + "_valued")
        self.own = sem(name + "_own")
        self.taken = sem(name + "_taken")

    def start_act(self, act):
        act.sem_inc(self.exped, 2)

    def start_dve(self, v):
        v.sem_inc(self.low, 2)

    def start_pe(self, pe):
        pe.sem_inc(self.valued, 1)
        pe.sem_inc(self.turned, TT)


    def pe_scores(self, pe, unit, i, q, k, extra=None):
        out = self.s_bank[i % 2]
        pe.wait_ge(self.exped, unit * TT + (i + 1))
        pairs = [(0, 0), (0, 1), (1, 0)]
        for n, (a, b) in enumerate(pairs):
            last = pe.matmul(out[:, :], q[a][:, i * P:(i + 1) * P], k[b], start=(n == 0),
                             stop=(n == 2 and extra is None), skip_group_check=True)
        if extra is not None:
            last = pe.matmul(out[:, i * P:T], extra[0], extra[1][:, 0:T - i * P], start=False, stop=True, skip_group_check=True)
        last.then_inc(self.scored, 1)

    def pe_turn(self, pe, unit, i, parity):
        if i == 0:
            pe.wait_ge(self.scaled, unit + 1)
        pe.wait_ge(self.low, unit * TT + (i + 1))
        out = self.t_bank[i % 2]
        for j in range(TT):
            last = pe.matmul(out[:, j * P:(j + 1) * P], self.probs[:, parity, i, j * P:(j + 1) * P], self.diag[:, i, :],
                             start=(j == 0), stop=(j == TT - 1), skip_group_check=True)
        last.then_inc(self.turned, 1)

    def pe_values(self, pe, unit, v):
        pe.wait_ge(self.low, unit * TT + (TT + 2))
        pe.wait_ge(self.taken, unit + 1)
        n = 0
        for j in range(TT):
            for a, b in ((0, 0), (0, 1), (1, 0)):
                last = pe.matmul(self.o_bank[:, :], v(a, j), self.pt[b][:, :, j, :], start=(n == 0), stop=(n == 3 * TT - 1))
                n += 1
        last.then_inc(self.valued, 1)

    def act_exp(self, act, unit, i, parity):
        act.wait_ge(self.peaked, unit * TT + (i + 1))
        act.activation(self.probs[:, parity, i, :], self.s_bank[i % 2][:, :], ACT.Exp, bias=self.shift[:, i:i + 1],
                       scale=self.scale, accum_out=self.sums[:, i:i + 1]).then_inc(self.exped, 1)

    def act_high(self, act, unit, i):
        act.wait_ge(self.turned, unit * TT + (TT + i + 1))
        if i == 0:
            act.wait_ge(self.valued, unit + 1)
        act.activation(self.pt[0][:, i], self.t_bank[i % 2][:, :].rearrange("p (j t) -> p j t", j=TT), ACT.Copy).then_inc(self.high, 1)

    def dve_peak(self, v, unit, i):
        v.wait_ge(self.scored, unit * TT + (i + 1))
        v.reduce_max(self.peak[:, i:i + 1], self.s_bank[i % 2][:, :], AX.X).then_inc(self.own, 1)
        v.wait_ge(self.own, unit * (TT + 1) + (i + 1))
        v.tensor_scalar(self.shift[:, i:i + 1], self.peak[:, i:i + 1], -self.scale, None, ALU.mult).then_inc(self.peaked, 1)

    def dve_scale(self, v, unit, identity):
        v.wait_ge(self.exped, unit * TT + (TT + 2))
        v.reciprocal(self.inverse[:, :], self.sums[:, :]).then_inc(self.own, 1)
        v.wait_ge(self.turned, unit * TT + TT)
        v.wait_ge(self.own, unit * (TT + 1) + (TT + 1))
        for i in range(TT):
            last = v.tensor_scalar(self.diag[:, i, :], identity, self.inverse[:, i:i + 1], None, ALU.mult)
        last.then_inc(self.scaled, 1)

    def dve_low(self, v, unit, i):
        v.wait_ge(self.high, unit * TT + (i + 1))
        v.tensor_tensor(self.pt[1][:, i], self.t_bank[i % 2][:, :].rearrange("p (j t) -> p j t", j=TT),
                        self.pt[0][:, i].bitcast(F32), ALU.subtract).then_inc(self.low, 1)


def pipeline(heads, scores, turn, values):
    for u in range(heads + 2):
        if u < heads:
            scores(u, 0)
            scores(u, 1)
        if u >= 2:
            values(u - 2)
        for i in range(TT):
            if 0 <= u - 1 < heads:
                turn(u - 1, i)
            if i < 2 and u < heads:
                scores(u, 2 + i)


PARTS = (0, 1)
PRODUCTS = ((0, 0), (0, 1), (1, 0))


def product(pe, out, weight, activation, chunks):
    n = 0
    for k in range(chunks):
        for a, b in PRODUCTS:
            last = pe.matmul(out, weight(a, k), activation(b, k), start=(n == 0), stop=(n == 3 * chunks - 1))
            n += 1
    return last


H0, DH0 = 16, 32
M0 = D // P
NEG_INF = -10000.0


def causal_phase(nc, io, x_dram, trace_dram, xa_dram):
    with ExitStack() as ctx:
        def sb(n, s, d=F32): return ctx.enter_context(nc.sbuf_tensor(n, s, d))
        def sem(n): return ctx.enter_context(nc.semaphore(n))
        core = Attention(nc, ctx, H0, 1.0, True)
        banks = [ctx.enter_context(nc.psum_tensor(f"p_bank{i}", [P, 512], F32)) for i in range(3)]
        identity = sb("ident2", [P, P])
        identity_r = sb("identity_r", [P, P], F32R)
        swap_r = sb("swap_r", [P, P], F32R)
        mask_r = sb("mask_r", [P, T], F32R)
        cos, sin = sb("cos", [P, T]), sb("sin", [P, T])
        qk_bias = sb("qk_bias", [P, 2 * M0])
        v_bias = sb("v_bias", [P, D])
        rows = sb("w_rows", [P, 2, D])
        wT = [sb(f"wT_{p}", [P, C, 3 * D], F32R) for p in ("hi", "lo")]
        tr = sb("tr", [P, C, T])
        tr_p = [sb(f"tr_{p}", [P, C, T], F32R) for p in ("hi", "lo")]
        xb = sb("xb", [P, C, T])
        u = sb("u", [P, 2, T])
        u_p = [sb(f"u_{p}", [P, 2, T], F32R) for p in ("hi", "lo")]
        turn_a, turn_b, turned = sb("turn_a", [P, 2, T]), sb("turn_b", [P, 2, T]), sb("turned", [P, 2, T])
        qk = [sb(f"qk_{p}", [P, 2 * M0, T], F32R) for p in ("hi", "lo")]
        vf = sb("vf", [P, 2, D])
        val = [sb(f"val_{p}", [P, TT, D], F32R) for p in ("hi", "lo")]
        s_const, s_w, s_cast, s_tr = sem("c_const"), [sem("c_w0"), sem("c_w1")], sem("c_cast"), sem("c_tr")
        s_wev, s_whi = sem("c_wev"), sem("c_whi")
        s_in = sem("c_in")
        s_split = sem("c_split")
        s_ahi = sem("c_ahi")
        s_proj = sem("c_proj")
        s_u = sem("c_u")
        s_uhi = sem("c_uhi")
        s_ulo = sem("c_ulo")
        s_swap = sem("c_swap")
        s_rot = sem("c_rot")
        s_rhi = sem("c_rhi")
        s_rlo = sem("c_rlo")
        s_vf, s_vhi, s_vlo = sem("c_vf"), sem("c_vhi"), sem("c_vlo")
        s_own = sem("c_own")
        s_out = sem("c_out")
        block = ctx.enter_context(nc.Block())
        w_tiles = io["L0_attn_Wqkv_w"].rearrange("(m p) k -> m p k", p=P)
        MT = 3 * D // P
        QK = 2 * M0
        LOADS = 7

        @block.sync
        def _(sp):
            for m in range(MT):
                if m >= 2:
                    sp.wait_ge(s_tr, m - 1)
                sp.dma_start(rows[:, m % 2, :], w_tiles[m]).then_inc(s_w[m % 2], 16)
            with sp.Fori(0, B) as b:
                sp.wait_ge(s_out, 16 * b + 16)
                sp.dma_start(tr[:, :, :], trace_dram[:, :, bass.ds(b, 1), :].rearrange("p c o t -> p c (o t)")).then_inc(s_in, 16)
                sp.dma_start(xb[:, :, :], x_dram[:, :, bass.ds(b, 1), :].rearrange("p c o t -> p c (o t)")).then_inc(s_in, 16)
                sp.wait_ge(core.taken, b * H0 + (H0 + 1))
                sp.dma_start(xa_dram[:, :, bass.ds(b, 1), :].rearrange("p c o t -> p c (o t)"), xb[:, :, :]).then_inc(s_out, 16)
            sp.wait_ge(s_out, 16 * B + 16)

        @block.gpsimd
        def _(g):
            g.dma_start(identity[:, :], io["const_identity"]).then_inc(s_const, 16)
            g.dma_start(identity_r[:, :], io["const_identity"]).then_inc(s_const, 16)
            g.dma_start(swap_r[:, :], io["const_swap"]).then_inc(s_const, 16)
            g.dma_start(mask_r[:, :], io["const_mask"]).then_inc(s_const, 16)
            g.dma_start(cos[:, :], io["const_cos"]).then_inc(s_const, 16)
            g.dma_start(sin[:, :], io["const_sin"]).then_inc(s_const, 16)
            with nc.allow_non_contiguous_dma(reason="1024 bias values, once"):
                g.dma_start(qk_bias[:, :], io["L0_attn_Wqkv_b"][0:2 * D].rearrange("(m p) -> p m", p=P)).then_inc(s_const, 16)
            g.dma_start(v_bias[:, :], io["L0_attn_Wqkv_b"][2 * D:3 * D].partition_broadcast(P)).then_inc(s_const, 16)

        @block.tensor
        def _(pe):
            core.start_pe(pe)
            pe.wait_ge(s_const, 128)
            for m in range(MT):
                pe.wait_ge(s_w[m % 2], 16 * (m // 2 + 1))
                if m >= 2:
                    pe.wait_ge(s_wev, m - 1)
                for k in range(C):
                    last = pe.matmul(banks[m % 2][:, k * P:(k + 1) * P], rows[:, m % 2, k * P:(k + 1) * P], identity[:, :],
                                     start=(k == 0), stop=(k == C - 1), skip_group_check=True)
                last.then_inc(s_tr, 1)
            pe.wait_ge(s_wev, MT)
            with pe.Fori(0, B) as b:
                pe.wait_ge(s_ahi, b + 1)
                pe.wait_ge(s_split, b + 1)

                def project(m):
                    pe.wait_ge(s_u, b * QK + (m + 1))
                    product(pe, banks[m % 2][:, :], lambda a, k: wT[a][:, k, m * P:(m + 1) * P],
                            lambda a, k: tr_p[a][:, k, :], C).then_inc(s_proj, 1)

                def swapped(m):
                    pe.wait_ge(s_ulo, b * QK + (m + 1))
                    pe.wait_ge(s_rot, b * QK + (m + 1))
                    pe.matmul(banks[2][:, :], swap_r[:, :], u_p[0][:, m % 2, :], start=True, stop=False)
                    pe.matmul(banks[2][:, :], swap_r[:, :], u_p[1][:, m % 2, :], start=False, stop=True).then_inc(s_swap, 1)

                project(0)
                for m in range(1, QK):
                    project(m)
                    swapped(m - 1)
                for i in range(TT):
                    if i < 2:
                        pe.wait_ge(s_u, b * QK + (QK + i + 1))
                    else:
                        pe.wait_ge(s_vf, b * TT + (i - 1))
                    n = 0
                    for k in range(C):
                        for a, c in PRODUCTS:
                            last = pe.matmul(banks[i % 2][:, :], tr_p[a][:, k, i * P:(i + 1) * P], wT[c][:, k, 2 * D:3 * D],
                                             start=(n == 0), stop=(n == 3 * C - 1))
                            n += 1
                    last.then_inc(s_proj, 1)
                    if i == 0:
                        swapped(QK - 1)
                pe.wait_ge(s_rlo, b * QK + QK)
                pe.wait_ge(s_vlo, b * TT + TT)

                def scores(h, i):
                    r, m = DH0 * (h % 4), h // 4
                    core.pe_scores(pe, b * H0 + h, i, [qk[a][r:r + DH0, m, :] for a in PARTS],
                                   [qk[a][r:r + DH0, M0 + m, :] for a in PARTS], extra=(identity_r[:, :], mask_r))

                pipeline(H0, scores, lambda h, i: core.pe_turn(pe, b * H0 + h, i, h % 2),
                         lambda h: core.pe_values(pe, b * H0 + h, lambda a, j: val[a][:, j, (h // 4) * P:(h // 4 + 1) * P]))

        @block.scalar
        def _(act):
            core.start_act(act)
            for m in range(MT):
                act.wait_ge(s_tr, m + 1)
                act.activation(wT[0][:, :, m * P:(m + 1) * P], banks[m % 2][:, :].rearrange("p (k o) -> p k o", k=C),
                               ACT.Copy).then_inc(s_whi, 1)
            act.sem_inc(s_u, 2)
            act.wait_ge(s_const, 128)
            with act.Fori(0, B) as b:
                act.wait_ge(s_in, 32 * b + 32)
                act.activation(tr_p[0][:, :, :], tr[:, :, :], ACT.Copy).then_inc(s_ahi, 1)

                def rotated_high(m):
                    act.wait_ge(s_rot, b * QK + (m + 2))
                    act.activation(qk[0][:, m, :], turned[:, m % 2, :], ACT.Copy).then_inc(s_rhi, 1)

                for m in range(QK):
                    act.wait_ge(s_proj, b * (QK + TT) + (m + 1))
                    act.activation(u[:, m % 2, :], banks[m % 2][:, :], ACT.Identity, bias=qk_bias[:, m:m + 1]).then_inc(s_u, 1)
                    act.wait_ge(s_u, b * QK + (m + 3))
                    act.wait_ge(s_swap, b * QK + (m - 1 + 2))
                    act.activation(u_p[0][:, m % 2, :], u[:, m % 2, :], ACT.Copy).then_inc(s_uhi, 1)
                    if m >= 1:
                        rotated_high(m - 1)
                rotated_high(QK - 1)
                for i in range(TT):
                    act.wait_ge(s_vf, b * TT + (i + 1))
                    act.activation(val[0][:, i, :], vf[:, i % 2, :], ACT.Copy).then_inc(s_vhi, 1)
                pipeline(H0, lambda h, i: core.act_exp(act, b * H0 + h, i, h % 2),
                         lambda h, i: core.act_high(act, b * H0 + h, i), lambda h: None)

        @block.vector
        def _(v):
            core.start_dve(v)
            v.sem_inc(core.taken, 1)
            v.sem_inc(s_rot, 1)
            v.sem_inc(s_out, 16)
            v.sem_inc(s_swap, 2)
            for m in range(MT):
                v.wait_ge(s_whi, m + 1)
                v.tensor_tensor(wT[1][:, :, m * P:(m + 1) * P], banks[m % 2][:, :].rearrange("p (k o) -> p k o", k=C),
                                wT[0][:, :, m * P:(m + 1) * P].bitcast(F32), ALU.subtract).then_inc(s_wev, 1)
            v.wait_ge(s_const, 128)
            with v.Fori(0, B) as b:
                v.wait_ge(s_ahi, b + 1)
                v.tensor_tensor(tr_p[1][:, :, :], tr[:, :, :], tr_p[0][:, :, :].bitcast(F32), ALU.subtract).then_inc(s_split, 1)
                scale = float(1.0 / np.sqrt(DH0))
                for m in range(QK):
                    w = m % 2
                    f = 1.0 if m < M0 else scale
                    v.wait_ge(s_uhi, b * QK + (m + 1))
                    v.tensor_tensor(u_p[1][:, w, :], u[:, w, :], u_p[0][:, w, :].bitcast(F32), ALU.subtract).then_inc(s_ulo, 1)
                    v.scalar_tensor_tensor(out=turn_a[:, w, :], in0=u[:, w, :], scalar=f, in1=cos[:, :], op0=ALU.mult, op1=ALU.mult)\
                        .then_inc(s_own, 1)
                    v.wait_ge(s_swap, b * QK + (m + 3))
                    v.scalar_tensor_tensor(out=turn_b[:, w, :], in0=banks[2][:, :], scalar=f, in1=sin[:, :], op0=ALU.mult, op1=ALU.mult)\
                        .then_inc(s_own, 1)
                    v.wait_ge(s_own, b * 2 * QK + (2 * m + 2))
                    v.tensor_tensor(turned[:, w, :], turn_a[:, w, :], turn_b[:, w, :], ALU.add).then_inc(s_rot, 1)
                    v.wait_ge(s_rhi, b * QK + (m + 1))
                    v.tensor_tensor(qk[1][:, m, :], turned[:, w, :], qk[0][:, m, :].bitcast(F32), ALU.subtract).then_inc(s_rlo, 1)
                for i in range(TT):
                    v.wait_ge(s_proj, b * (QK + TT) + (QK + i + 1))
                    v.tensor_tensor(vf[:, i % 2, :], banks[i % 2][:, :], v_bias[:, :], ALU.add).then_inc(s_vf, 1)
                    v.wait_ge(s_vhi, b * TT + (i + 1))
                    v.tensor_tensor(val[1][:, i, :], vf[:, i % 2, :], val[0][:, i, :].bitcast(F32), ALU.subtract).then_inc(s_vlo, 1)

                def take(h):
                    r, m = DH0 * (h % 4), h // 4
                    v.wait_ge(core.valued, b * H0 + (h + 2))
                    v.tensor_tensor(xb[r:r + DH0, m, :], xb[r:r + DH0, m, :], core.o_bank[r:r + DH0, :], ALU.add)\
                        .then_inc(core.taken, 1)

                def low(h, i):
                    core.dve_low(v, b * H0 + h, i)

                dve_pipeline(core, v, b * H0, H0, low, take, identity)


def dve_pipeline(core, v, first, heads, low, take, identity):
    for u in range(heads + 2):
        if u < heads:
            core.dve_peak(v, first + u, 0)
            core.dve_peak(v, first + u, 1)
        if u >= 2:
            take(u - 2)
        for i in range(TT):
            if 0 <= u - 1 < heads:
                low(u - 1, i)
            if i < 2 and u < heads:
                core.dve_peak(v, first + u, 2 + i)
        if u < heads:
            core.dve_scale(v, first + u, identity[:, :])


ADA = 6 * D // P
SHIFT1, SCALE1, GATE1, SHIFT2, SCALE2, GATE2 = (C * i for i in range(6))
LN_EPS = 1e-6


def row_of(dram, b):
    return dram[:, :, bass.ds(b, 1), :].rearrange("p c o t -> p c (o t)")


def ada_phase(nc, io, cond_dram, ada_dram):
    with ExitStack() as ctx:
        def sb(n, s, d=F32): return ctx.enter_context(nc.sbuf_tensor(n, s, d))
        def sem(n): return ctx.enter_context(nc.semaphore(n))
        QUARTERS = 4
        w = [sb(f"ada_w{i}", [P, C, 6 * D // QUARTERS]) for i in range(QUARTERS)]
        cond = sb("ada_cond", [P, C, B])
        bias = sb("ada_bias", [P, ADA])
        ada = sb("ada", [P, ADA, B])
        bank = ctx.enter_context(nc.psum_tensor("ada_bank", [P, 512], F32))
        s_w = [sem(f"a_w{i}") for i in range(QUARTERS)]
        s_small, s_mm, s_add, s_out = sem("a_small"), sem("a_mm"), sem("a_add"), sem("a_out")
        block = ctx.enter_context(nc.Block())
        w_view = io["L0_cond2_ada_w"].rearrange("(c p) n -> p c n", p=P)

        @block.sync
        def _(sp):
            sp.dma_start(cond[:, :, :], cond_dram).then_inc(s_small, 16)
            for i in range(QUARTERS):
                sp.dma_start(w[i][:, :, :], w_view[:, :, i * 768:(i + 1) * 768]).then_inc(s_w[i], 16)
            sp.wait_ge(s_add, 1)
            sp.dma_start(ada_dram, ada[:, :, :]).then_inc(s_out, 16)
            sp.wait_ge(s_out, 16)

        @block.scalar
        def _(act):
            with nc.allow_non_contiguous_dma(reason="the bias, once"):
                act.dma_start(bias[:, :], io["L0_cond2_ada_b"].rearrange("(m p) -> p m", p=P)).then_inc(s_small, 16)

        @block.tensor
        def _(pe):
            pe.wait_ge(s_small, 32)
            per = ADA // QUARTERS
            for m in range(ADA):
                if m % per == 0:
                    pe.wait_ge(s_w[m // per], 16)
                for k in range(C):
                    last = pe.matmul(bank[:, m * B:(m + 1) * B], w[m // per][:, k, (m % per) * P:(m % per + 1) * P], cond[:, k, :],
                                     start=(m == 0 and k == 0), stop=(m == ADA - 1 and k == C - 1), skip_group_check=True)
            last.then_inc(s_mm, 1)

        @block.vector
        def _(v):
            v.wait_ge(s_mm, 1)
            for b in range(B):
                last = v.tensor_tensor(ada[:, :, b], bank[:, 0:ADA * B].rearrange("p (m b) -> p m b", b=B)[:, :, b], bias[:, :], ALU.add)
            last.then_inc(s_add, 1)


def norm_phase(nc, io, tag, x_dram, ada_dram, shift, scale, gate, bias_name, parts_dram, carried_dram):
    with ExitStack() as ctx:
        def sb(n, s, d=F32): return ctx.enter_context(nc.sbuf_tensor(tag + n, s, d))
        def sem(n): return ctx.enter_context(nc.semaphore(tag + n))
        x = sb("x", [P, 2, C, T])
        x_p = [sb(f"x{p}", [P, 2, C, T], F32R) for p in PARTS]
        sq = sb("sq", [P, C, T])
        centred = sb("centred", [P, C, T])
        out = sb("out", [P, C, T])
        out_p = [sb(f"out{p}", [P, 2, C, T], F32R) for p in PARTS]
        carried = sb("carried", [P, 2, C, T])
        ada = sb("ada", [P, ADA, B])
        one_plus = sb("one_plus", [P, C, B])
        bias = sb("bias", [P, C])
        gated = sb("gated", [P, C, B])
        mean_f, mean_w = sb("mean_f", [P, P]), sb("mean_w", [P, P], F32R)
        eps = sb("eps", [P, 1])
        dev, inv, var, t1, t2, rstd = [sb(n, [P, T]) for n in ("dev", "inv", "var", "t1", "t2", "rstd")]
        banks = [ctx.enter_context(nc.psum_tensor(f"{tag}bank{i}", [P, 512], F32)) for i in range(2)]
        s_x = [sem("s_x0"), sem("s_x1")]
        s_small, s_pre, s_own = sem("s_small"), sem("s_pre"), sem("s_own")
        s_hi = sem("s_hi")
        s_lo = sem("s_lo")
        s_mm = sem("s_mm")
        s_c, s_sq, s_dev, s_scaled, s_shifted, s_car = [sem("s_" + n) for n in ("c", "sq", "dev", "scaled", "shifted", "car")]
        s_out = [sem("s_out0"), sem("s_out1")]
        block = ctx.enter_context(nc.Block())

        @block.sync
        def _(sp):
            for b in range(B):
                if b >= 2:
                    sp.wait_ge(s_c, b - 1)
                    sp.wait_ge(s_car, b - 1)
                sp.dma_start(x[:, b % 2], row_of(x_dram, b)).then_inc(s_x[b % 2], 16)
            for b in range(B):
                sp.wait_ge(s_lo, 3 * b + 3)
                sp.wait_ge(s_car, b + 1)
                for p in PARTS:
                    sp.dma_start(row_of(parts_dram[p], b), out_p[p][:, b % 2].bitcast(F32)).then_inc(s_out[b % 2], 16)
                sp.dma_start(row_of(carried_dram, b), carried[:, b % 2]).then_inc(s_out[b % 2], 16)
            for i in range(2):
                sp.wait_ge(s_out[i], 48 * 2)

        @block.scalar
        def _(act):
            act.dma_start(ada[:, :, :], ada_dram).then_inc(s_small, 16)
            with nc.allow_non_contiguous_dma(reason="512 bias values, once"):
                act.dma_start(bias[:, :], io[bias_name].rearrange("(c p) -> p c", p=P)).then_inc(s_small, 16)
            act.wait_ge(s_pre, 1)
            for b in range(B):
                w = b % 2
                act.wait_ge(s_x[w], 16 * (b // 2 + 1))
                if b >= 2:
                    act.wait_ge(s_mm, 2 * (b - 2) + 1)
                act.activation(x_p[0][:, w], x[:, w], ACT.Copy).then_inc(s_hi, 1)
                act.wait_ge(s_c, b + 1)
                act.activation(sq[:, :, :], centred[:, :, :], ACT.Square).then_inc(s_sq, 1)
                act.wait_ge(s_sq, b + 1)
                act.wait_ge(s_mm, 2 * b + 1)
                act.activation(x_p[0][:, w], sq[:, :, :], ACT.Copy).then_inc(s_hi, 1)
                act.wait_ge(s_mm, 2 * b + 2)
                act.activation(dev[:, :], banks[1][:, :], ACT.Sqrt, bias=eps[:, :]).then_inc(s_dev, 1)
                act.wait_ge(s_scaled, b + 1)
                for c in range(C):
                    last = act.activation(out[:, c, :], centred[:, c, :], ACT.Identity, bias=ada[:, shift + c, b:b + 1])
                last.then_inc(s_shifted, 1)
                act.wait_ge(s_shifted, b + 1)
                if b >= 2:
                    act.wait_ge(s_out[w], 48 * (b // 2))
                act.activation(out_p[0][:, w], out[:, :, :], ACT.Copy).then_inc(s_hi, 1)

        @block.tensor
        def _(pe):
            pe.wait_ge(s_pre, 2)
            for b in range(B):
                for j in range(2):
                    pe.wait_ge(s_lo, 3 * b + j + 1)
                    n = 0
                    for k in range(C):
                        for p in PARTS:
                            last = pe.matmul(banks[j][:, :], mean_w[:, :], x_p[p][:, b % 2, k, :], start=(n == 0), stop=(n == 2 * C - 1))
                            n += 1
                    last.then_inc(s_mm, 1)

        @block.vector
        def _(v):
            v.memset(mean_f[:, :], 1.0 / D).then_inc(s_own, 1)
            v.memset(eps[:, :], LN_EPS).then_inc(s_pre, 1)
            v.wait_ge(s_own, 1)
            v.tensor_copy(mean_w[:, :], mean_f[:, :]).then_inc(s_pre, 1)
            v.wait_ge(s_small, 32)
            v.tensor_scalar(one_plus[:, :, :], ada[:, scale:scale + C, :], 1.0, None, ALU.add).then_inc(s_own, 1)
            for b in range(B):
                last = v.tensor_tensor(gated[:, :, b], ada[:, gate:gate + C, b], bias[:, :], ALU.mult)
            last.then_inc(s_own, 1)
            n = 3
            v.wait_ge(s_own, n)

            def own(ins):
                nonlocal n
                ins.then_inc(s_own, 1)
                n += 1
                v.wait_ge(s_own, n)

            for b in range(B):
                w = b % 2
                v.wait_ge(s_hi, 3 * b + 1)
                v.tensor_tensor(x_p[1][:, w], x[:, w], x_p[0][:, w].bitcast(F32), ALU.subtract).then_inc(s_lo, 1)
                if b >= 2:
                    v.wait_ge(s_out[w], 48 * (b // 2))
                for c in range(C):
                    last = v.tensor_scalar(carried[:, w, c, :], x[:, w, c, :], gated[:, c, b:b + 1], None, ALU.add)
                last.then_inc(s_car, 1)
                v.wait_ge(s_mm, 2 * b + 1)
                if b >= 1:
                    v.wait_ge(s_shifted, b)
                for c in range(C):
                    last = v.tensor_tensor(centred[:, c, :], x[:, w, c, :], banks[0][:, :], ALU.subtract)
                last.then_inc(s_c, 1)
                v.wait_ge(s_hi, 3 * b + 2)
                v.tensor_tensor(x_p[1][:, w], sq[:, :, :], x_p[0][:, w].bitcast(F32), ALU.subtract).then_inc(s_lo, 1)
                v.wait_ge(s_dev, b + 1)
                v.tensor_scalar(var[:, :], banks[1][:, :], LN_EPS, None, ALU.add)
                own(v.reciprocal(inv[:, :], dev[:, :]))
                own(v.tensor_tensor(t1[:, :], inv[:, :], inv[:, :], ALU.mult))
                own(v.scalar_tensor_tensor(out=t2[:, :], in0=t1[:, :], scalar=-0.5, in1=var[:, :], op0=ALU.mult, op1=ALU.mult))
                own(v.scalar_tensor_tensor(out=rstd[:, :], in0=t2[:, :], scalar=1.5, in1=inv[:, :], op0=ALU.add, op1=ALU.mult))
                for c in range(C):
                    last = v.scalar_tensor_tensor(out=centred[:, c, :], in0=centred[:, c, :], scalar=one_plus[:, c, b:b + 1],
                                                  in1=rstd[:, :], op0=ALU.mult, op1=ALU.mult)
                last.then_inc(s_scaled, 1)
                v.wait_ge(s_hi, 3 * b + 3)
                v.tensor_tensor(out_p[1][:, w], out[:, :, :], out_p[0][:, w].bitcast(F32), ALU.subtract).then_inc(s_lo, 1)


H1, DH1 = 16, 128
GROUP = 4
GROUPS = H1 // GROUP
INNER = H1 * DH1
V_, Q_, K_, O_ = range(4)


def attention_phase(nc, io, parts_dram, ada_dram, carried_dram):
    with ExitStack() as ctx:
        def sb(n, s, d=F32): return ctx.enter_context(nc.sbuf_tensor("t_" + n, s, d))
        def sem(n): return ctx.enter_context(nc.semaphore("t_" + n))
        core = Attention(nc, ctx, GROUP, float(DH1) ** -0.5, False)
        banks = [ctx.enter_context(nc.psum_tensor(f"t_bank{i}", [P, 512], F32)) for i in range(3)]
        identity = sb("ident", [P, P])
        x_p = [sb(f"x{p}", [P, C, T], F32R) for p in PARTS]
        raw = sb("raw", [P, 2, C, 512])
        weight = [[sb(f"w{i}{p}", [P, C, 512], F32R) for p in PARTS] for i in range(4)]
        q_p = [sb(f"q{p}", [P, GROUP, T], F32R) for p in PARTS]
        k_p = [sb(f"k{p}", [P, GROUP, T], F32R) for p in PARTS]
        val = [sb(f"v{p}", [P, TT, GROUP * DH1], F32R) for p in PARTS]
        att = [sb(f"a{p}", [P, GROUP, T], F32R) for p in PARTS]
        carried = sb("carried", [P, C, T])
        ada = sb("ada", [P, ADA, B])
        bias = sb("bias", [P, 3, H1])
        bias_now = sb("bias_now", [P, 3, GROUP])
        gate_now = sb("gate_now", [P, C])
        s_small = sem("small")
        s_raw = [sem("raw0"), sem("raw1")]
        s_whi = sem("whi")
        s_wlo = sem("wlo")
        s_x = sem("x")
        s_now = sem("now")
        s_proj = sem("proj")
        s_uhi = sem("uhi")
        s_ulo = sem("ulo")
        s_ahi = sem("ahi")
        s_car = sem("car")
        s_o = sem("o")
        s_added = sem("added")
        s_turn = sem("turn")
        s_back = sem("back")
        block = ctx.enter_context(nc.Block())
        N = B * GROUPS
        TILES = 3 * GROUP
        qkv_w = io["L0_cond2_qkv_w"].rearrange("(c p) n -> p c n", p=P)
        out_w = io["L0_cond2_out_w"].rearrange("(h p) n -> p h n", p=P)

        def place(i, group):
            return group * GROUP if i == O_ else group * 512 + {Q_: 0, K_: 1, V_: 2}[i] * INNER

        def source(i, at):
            return out_w[:, bass.ds(at, GROUP), :] if i == O_ else qkv_w[:, :, bass.ds(at, 512)]

        @block.sync
        def _(sp):
            def load_row(row):
                for p in PARTS:
                    sp.dma_start(x_p[p][:, :, :].bitcast(F32), row_of(parts_dram[p], row)).then_inc(s_x, 16)

            for n, i in enumerate((V_, Q_)):
                sp.dma_start(raw[:, n % 2], source(i, place(i, 0))).then_inc(s_raw[n % 2], 16)
            load_row(0)
            sp.wait_ge(s_wlo, 3)
            sp.dma_start(raw[:, 0], source(K_, place(K_, 0))).then_inc(s_raw[0], 16)
            with sp.Fori(0, N) as it:
                following = (it + 1) % N
                row, next_row = sp.snap(it // GROUPS), sp.snap(following // GROUPS)
                at = {i: sp.snap(place(i, (it if i == O_ else following) % GROUPS)) for i in (O_, V_, Q_, K_)}
                sp.wait_ge(s_back, 16 * it + 16)
                sp.dma_start(carried[:, :, :], row_of(carried_dram, row)).then_inc(s_car, 16)
                for j, i in enumerate((O_, V_, Q_, K_)):
                    if i == V_:
                        sp.wait_ge(s_proj, it * TILES + TILES)
                        load_row(next_row)
                    sp.wait_ge(s_wlo, it * 4 + (3 + j + 1))
                    sp.sem_inc(s_turn, 1)
                    sp.dma_start(raw[:, (3 + j) % 2], source(i, at[i])).then_inc(s_raw[(3 + j) % 2], 16)
                sp.wait_ge(s_added, it * C + (C + 2))
                sp.dma_start(row_of(carried_dram, row), carried[:, :, :]).then_inc(s_back, 16)
            sp.wait_ge(s_back, 16 * N + 16)

        @block.gpsimd
        def _(g):
            g.sem_inc(s_wlo, 2)
            g.dma_start(identity[:, :], io["const_identity"]).then_inc(s_small, 16)
            g.dma_start(ada[:, :, :], ada_dram).then_inc(s_small, 16)
            with nc.allow_non_contiguous_dma(reason="6144 bias values, once"):
                g.dma_start(bias[:, :, :], io["L0_cond2_qkv_b"].rearrange("(s m p) -> p s m", s=3, p=P)).then_inc(s_small, 16)

            for n, i in enumerate((V_, Q_, K_)):
                g.wait_ge(s_whi, n + 1)
                g.tensor_tensor(weight[i][1][:, :, :], raw[:, n % 2], weight[i][0][:, :, :].bitcast(F32), ALU.subtract).then_inc(s_wlo, 1)
            with g.Fori(0, N) as it:
                for j, i in enumerate((O_, V_, Q_, K_)):
                    g.wait_ge(s_whi, it * 4 + (3 + j + 1))
                    g.tensor_tensor(weight[i][1][:, :, :], raw[:, (3 + j) % 2], weight[i][0][:, :, :].bitcast(F32), ALU.subtract).then_inc(s_wlo, 1)

        def weight_high(act, it, j):
            i = (O_, V_, Q_, K_)[j]
            which = (3 + j) % 2
            before = 2 if which == 0 else 1
            act.wait_ge(s_raw[which], it * 32 + 16 * (before + j // 2 + 1))
            if i == O_:
                act.wait_ge(s_o, it * C + C)
            else:
                act.wait_ge(s_proj, it * TILES + (GROUP if i == V_ else TILES))
            act.activation(weight[i][0][:, :, :], raw[:, which], ACT.Copy).then_inc(s_whi, 1)

        @block.scalar
        def _(act):
            core.start_act(act)
            for n, i in enumerate((V_, Q_, K_)):
                act.wait_ge(s_raw[n % 2], 16 * (n // 2 + 1))
                act.activation(weight[i][0][:, :, :], raw[:, n % 2], ACT.Copy).then_inc(s_whi, 1)
            with act.Fori(0, N) as it:
                act.wait_ge(s_now, it + 1)
                for n in range(TILES):
                    act.wait_ge(s_proj, it * TILES + (n + 1))
                    if n < GROUP:
                        act.activation(val[0][:, n, :], banks[n % 2][:, :], ACT.Copy).then_inc(s_uhi, 1)
                    else:
                        s, h = (n - GROUP) % 2, (n - GROUP) // 2
                        act.activation((q_p, k_p)[s][0][:, h, :], banks[n % 2][:, :], ACT.Identity,
                                       bias=bias_now[:, s, h:h + 1]).then_inc(s_uhi, 1)

                def take(h):
                    act.wait_ge(core.valued, it * GROUP + (h + 2))
                    act.activation(att[0][:, h, :], core.o_bank[:, :], ACT.Identity, bias=bias_now[:, 2, h:h + 1]).then_inc(s_ahi, 1)

                order = iter(range(4))

                def high(h, i):
                    core.act_high(act, it * GROUP + h, i)
                    if i == TT - 1:
                        weight_high(act, it, next(order))

                pipeline(GROUP, lambda h, i: core.act_exp(act, it * GROUP + h, i, h % 2), high, take)

        @block.tensor
        def _(pe):
            core.start_pe(pe)
            pe.sem_inc(s_o, C)
            pe.wait_ge(s_small, 48)
            with pe.Fori(0, N) as it:
                pe.wait_ge(s_x, 32 * it + 32)
                pe.wait_ge(s_added, it * C + 2)
                pe.wait_ge(s_wlo, it * 4 + 3)
                for i in range(TT):
                    pe.wait_ge(s_ulo, it * TILES + (i + 1))
                    n = 0
                    for k in range(C):
                        for a, c in PRODUCTS:
                            last = pe.matmul(banks[i % 2][:, :], x_p[a][:, k, i * P:(i + 1) * P], weight[V_][c][:, k, :],
                                             start=(n == 0), stop=(n == 3 * C - 1))
                            n += 1
                    last.then_inc(s_proj, 1)
                pe.wait_ge(s_wlo, it * 4 + 5)
                for n in range(GROUP, TILES):
                    s, h = (n - GROUP) % 2, (n - GROUP) // 2
                    w = weight[(Q_, K_)[s]]
                    pe.wait_ge(s_ulo, it * TILES + (n + 1))
                    last = product(pe, banks[n % 2][:, :], lambda a, k: w[a][:, k, h * P:(h + 1) * P], lambda a, k: x_p[a][:, k, :], C)
                    last.then_inc(s_proj, 1)
                pe.wait_ge(s_ulo, it * TILES + (TILES + 2))
                pipeline(GROUP,
                         lambda h, i: core.pe_scores(pe, it * GROUP + h, i, [q_p[a][:, h, :] for a in PARTS], [k_p[a][:, h, :] for a in PARTS]),
                         lambda h, i: core.pe_turn(pe, it * GROUP + h, i, h % 2),
                         lambda h: core.pe_values(pe, it * GROUP + h, lambda a, j: val[a][:, j, h * DH1:(h + 1) * DH1]))
                pe.wait_ge(core.taken, it * GROUP + (GROUP + 1))
                pe.wait_ge(s_wlo, it * 4 + 6)
                for m in range(C):
                    pe.wait_ge(s_added, it * C + (m + 1))
                    last = product(pe, banks[m % 2][:, :], lambda a, k: weight[O_][a][:, k, m * P:(m + 1) * P], lambda a, k: att[a][:, k, :], GROUP)
                    last.then_inc(s_o, 1)

        @block.vector
        def _(v):
            core.start_dve(v)
            v.sem_inc(core.taken, 1)
            v.sem_inc(s_ulo, 2)
            v.sem_inc(s_added, 2)
            v.sem_inc(s_back, 16)
            v.wait_ge(s_small, 48)
            with v.Fori(0, N) as it:
                v.wait_ge(core.valued, it * GROUP + 1)
                v.wait_ge(s_added, it * C + 2)
                v.tensor_copy(gate_now[:, :], ada[:, GATE1:GATE1 + C, bass.ds(it // GROUPS, 1)].rearrange("p c o -> p (c o)"))
                v.tensor_copy(bias_now[:, :, :], bias[:, :, bass.ds((it % GROUPS) * GROUP, GROUP)]).then_inc(s_now, 1)
                v.wait_ge(s_now, it + 1)
                for n in range(TILES):
                    v.wait_ge(s_uhi, it * TILES + (n + 1))
                    if n < GROUP:
                        v.tensor_tensor(val[1][:, n, :], banks[n % 2][:, :], val[0][:, n, :].bitcast(F32), ALU.subtract).then_inc(s_ulo, 1)
                    else:
                        s, h = (n - GROUP) % 2, (n - GROUP) // 2
                        hi, lo = [(q_p, k_p)[s][p][:, h, :] for p in PARTS]
                        v.scalar_tensor_tensor(out=lo, in0=banks[n % 2][:, :], scalar=bias_now[:, s, h:h + 1], in1=hi.bitcast(F32),
                                               op0=ALU.add, op1=ALU.subtract).then_inc(s_ulo, 1)

                def take(h):
                    v.wait_ge(s_ahi, it * GROUP + (h + 1))
                    v.scalar_tensor_tensor(out=att[1][:, h, :], in0=core.o_bank[:, :], scalar=bias_now[:, 2, h:h + 1],
                                           in1=att[0][:, h, :].bitcast(F32), op0=ALU.add, op1=ALU.subtract).then_inc(core.taken, 1)

                dve_pipeline(core, v, it * GROUP, GROUP, lambda h, i: core.dve_low(v, it * GROUP + h, i), take, identity)
                v.wait_ge(s_car, 16 * it + 16)
                for m in range(C):
                    v.wait_ge(s_o, it * C + (C + m + 1))
                    v.scalar_tensor_tensor(out=carried[:, m, :], in0=banks[m % 2][:, :], scalar=gate_now[:, m:m + 1],
                                           in1=carried[:, m, :], op0=ALU.mult, op1=ALU.add).then_inc(s_added, 1)


HIDDEN = 4 * D
HT = HIDDEN // P


def ffn_phase(nc, io, sign, parts_dram, ada_dram, base_dram, result):
    with ExitStack() as ctx:
        tag = "b_" if sign else "g_"
        def sb(n, s, d=F32): return ctx.enter_context(nc.sbuf_tensor(tag + n, s, d))
        def sem(n): return ctx.enter_context(nc.semaphore(tag + n))
        WP = (0,) if sign else PARTS
        CHUNK = 4
        raw = sb("raw", [P, 2, CHUNK, 512])
        w1 = [sb(f"w1{p}", [P, C, HIDDEN], F32R) for p in WP]
        w2 = [sb(f"w2{p}", [P, HT, D], F32R) for p in WP]
        x_p = [sb(f"x{p}", [P, C, T], F32R) for p in PARTS]
        h = sb("h", [P, 2, T])
        h_p = [sb(f"h{p}", [P, 2, T], F32R) for p in PARTS]
        base = sb("base", [P, C, T])
        per_hidden = sb("per_hidden", [P, HT])
        identity = sb("ident", [P, P])
        acc = [ctx.enter_context(nc.psum_tensor(f"{tag}acc{i}", [P, 512], F32)) for i in range(C)]
        hb = [ctx.enter_context(nc.psum_tensor(f"{tag}hb{i}", [P, 512], F32)) for i in range(2)]
        s_small = sem("small")
        s_raw = [sem("raw0"), sem("raw1")]
        s_tr, s_whi, s_wlo = sem("tr"), sem("whi"), sem("wlo")
        s_x, s_xp, s_base = sem("x"), sem("xp"), sem("base")
        s_h = sem("h")
        s_act = sem("act")
        s_hhi = sem("hhi")
        s_hlo = sem("hlo")
        s_used = sem("used")
        s_done = sem("done")
        s_out = sem("out")
        s_own = sem("own")
        gate = sb("gate", [P, C, B])
        gate_now = sb("gate_now", [P, C])
        if sign:
            x32 = sb("x32", [P, C, T])
            final = sb("final", [P, C, T])
            tokens = sb("tokens", [P, 2, D])
            down_scale, output_scale = sb("down_scale", [P, C]), sb("output_scale", [P, 1])
            s_tt, s_tok, s_sent = sem("tt"), sem("tok"), [sem("sent0"), sem("sent1")]
            tb = [ctx.enter_context(nc.psum_tensor(f"{tag}tb{i}", [P, 512], F32)) for i in range(2)]
            loads = [io["L0_ffn_up_weight"][512 * i:512 * (i + 1), :].rearrange("(c p) n -> p c n", p=P) for i in range(4)]
            loads += [io["L0_ffn_down_weight"].rearrange("(c p) n -> p c n", p=P)[:, :, 512 * i:512 * (i + 1)] for i in range(4)]
        else:
            ada = sb("ada", [P, ADA, B])
            loads = [io["L0_cond2_ffn_w1"].rearrange("(c p) n -> p c n", p=P)[:, :, 512 * i:512 * (i + 1)] for i in range(4)]
            loads += [io["L0_cond2_ffn_w2"][512 * i:512 * (i + 1), :].rearrange("(c p) n -> p c n", p=P) for i in range(4)]
        NL = len(loads)
        block = ctx.enter_context(nc.Block())

        def part(p, n):
            return w1[p][:, :, 512 * n:512 * (n + 1)] if n < 4 else w2[p][:, 4 * (n - 4):4 * (n - 3), :]

        @block.sync
        def _(sp):
            for n in range(NL):
                if n >= 2:
                    sp.wait_ge(s_tr if sign else s_wlo, 4 * (n - 1) if sign else n - 1)
                sp.dma_start(raw[:, n % 2], loads[n]).then_inc(s_raw[n % 2], 16)
            with sp.Fori(0, B) as b:
                if sign:
                    sp.wait_ge(s_done, b * C + C)
                else:
                    sp.wait_ge(s_out, 16 * b + 16)
                sp.dma_start(base[:, :, :], row_of(base_dram, b)).then_inc(s_base, 16)
                if not sign:
                    sp.wait_ge(s_done, b * C + (2 * C))
                    sp.dma_start(row_of(result, b), base[:, :, :]).then_inc(s_out, 16)
                else:
                    for i in range(TT):
                        sp.wait_ge(s_tok, b * TT + (i + 3))
                        sp.dma_start(result[bass.ds(b, 1), i * P:(i + 1) * P, :].rearrange("o p n -> (o p) n"), tokens[:, i % 2, :]).then_inc(s_sent[i % 2], 16)
            if sign:
                for i in range(2):
                    sp.wait_ge(s_sent[i], 16 * (B * TT // 2) + 16)
            else:
                sp.wait_ge(s_out, 16 * B + 16)

        @block.gpsimd
        def _(g):
            g.dma_start(identity[:, :], io["const_identity"]).then_inc(s_small, 16)
            with nc.allow_non_contiguous_dma(reason="2048 values, once"):
                g.dma_start(per_hidden[:, :], io["L0_ffn_up_scale" if sign else "L0_cond2_ffn_b1"].rearrange("(m p) -> p m", p=P)).then_inc(s_small, 16)
                if sign:
                    g.dma_start(down_scale[:, :], io["L0_ffn_down_scale"].rearrange("(c p) -> p c", p=P)).then_inc(s_small, 16)
                    g.dma_start(output_scale[:, :], io["L0_ffn_output_scale"].partition_broadcast(P)).then_inc(s_small, 16)
                else:
                    g.dma_start(ada[:, :, :], ada_dram).then_inc(s_small, 32)
            with g.Fori(0, B) as b:
                g.wait_ge(s_act, b * HT + 2)
                if sign:
                    g.dma_start(x32[:, :, :], row_of(parts_dram[0], b)).then_inc(s_x, 32)
                else:
                    for p in PARTS:
                        g.dma_start(x_p[p][:, :, :].bitcast(F32), row_of(parts_dram[p], b)).then_inc(s_x, 16)

        @block.tensor
        def _(pe):
            pe.sem_inc(s_used, 2)
            pe.wait_ge(s_small, 64)
            if sign:
                for n in range(NL):
                    pe.wait_ge(s_raw[n % 2], 16 * (n // 2 + 1))
                    for r in range(4):
                        q = 4 * n + r
                        if q >= 2:
                            pe.wait_ge(s_whi, q - 1)
                        for c in range(4):
                            last = pe.matmul(tb[q % 2][:, c * P:(c + 1) * P], raw[:, n % 2, c, r * P:(r + 1) * P], identity[:, :],
                                             start=(c == 0), stop=(c == 3), skip_group_check=True)
                        last.then_inc(s_tr, 1)
                pe.wait_ge(s_whi, 4 * NL)
            else:
                pe.wait_ge(s_wlo, NL)
            with pe.Fori(0, B) as b:
                if sign:
                    pe.wait_ge(s_xp, 2 * b + 2)
                else:
                    pe.wait_ge(s_x, 32 * b + 32)

                def hidden(j):
                    pe.wait_ge(s_act, b * HT + (j + 1))
                    n, total = 0, C * (2 if sign else 3)
                    for k in range(C):
                        for a, c in (((0, 0), (0, 1)) if sign else PRODUCTS):
                            last = pe.matmul(hb[j % 2][:, :], w1[a][:, k, j * P:(j + 1) * P], x_p[c][:, k, :], start=(n == 0), stop=(n == total - 1))
                            n += 1
                    last.then_inc(s_h, 1)

                def output(j):
                    if j == 0:
                        pe.wait_ge(s_done, b * C + C)
                    pe.wait_ge(s_hlo, b * HT + (j + 1))
                    pairs = ((0, 0), (0, 1)) if sign else PRODUCTS
                    for m in range(C):
                        for i, (a, c) in enumerate(pairs):
                            last = pe.matmul(acc[m][:, :], w2[a][:, j, m * P:(m + 1) * P], h_p[c][:, j % 2, :],
                                             start=(j == 0 and i == 0), stop=(j == HT - 1 and i == len(pairs) - 1))
                    last.then_inc(s_used, 1)

                hidden(0)
                for j in range(1, HT):
                    hidden(j)
                    output(j - 1)
                output(HT - 1)
                if sign:
                    pe.wait_ge(s_done, b * C + 2 * C)
                    for i in range(TT):
                        pe.wait_ge(s_tok, b * TT + (i + 1))
                        for c in range(C):
                            last = pe.matmul(tb[i % 2][:, c * P:(c + 1) * P], final[:, c, i * P:(i + 1) * P], identity[:, :],
                                             start=(c == 0), stop=(c == C - 1), skip_group_check=True)
                        last.then_inc(s_tt, 1)

        @block.scalar
        def _(act):
            act.sem_inc(s_act, 2)
            if sign:
                for q in range(4 * NL):
                    n, r = q // 4, q % 4
                    act.wait_ge(s_tr, q + 1)
                    dst = w1[0][:, r, 512 * n:512 * (n + 1)] if n < 4 else w2[0][:, 4 * (n - 4) + r, :]
                    act.activation(dst, tb[q % 2][:, :], ACT.Sign).then_inc(s_whi, 1)
            else:
                for n in range(NL):
                    act.wait_ge(s_raw[n % 2], 16 * (n // 2 + 1))
                    act.activation(part(0, n), raw[:, n % 2], ACT.Copy).then_inc(s_whi, 1)
            act.wait_ge(s_small, 64)
            with act.Fori(0, B) as b:
                if sign:
                    act.wait_ge(s_x, 32 * b + 32)
                    act.activation(x_p[0][:, :, :], x32[:, :, :], ACT.Copy).then_inc(s_xp, 1)
                for j in range(HT):
                    act.wait_ge(s_h, b * HT + (j + 1))
                    if j >= 2:
                        act.wait_ge(s_hlo, b * HT + (j - 1))
                    if sign:
                        act.activation(h[:, j % 2, :], hb[j % 2][:, :], ACT.Relu, scale=per_hidden[:, j:j + 1]).then_inc(s_act, 1)
                    else:
                        act.activation(h[:, j % 2, :], hb[j % 2][:, :], ACT.Gelu, bias=per_hidden[:, j:j + 1]).then_inc(s_act, 1)
                    act.wait_ge(s_act, b * HT + (j + 3))
                    act.wait_ge(s_used, b * HT + (j + 1))
                    act.activation(h_p[0][:, j % 2, :], h[:, j % 2, :], ACT.Copy).then_inc(s_hhi, 1)

        @block.vector
        def _(v):
            v.sem_inc(s_done, C)
            v.sem_inc(s_out, 16)
            if sign:
                v.sem_inc(s_tok, 2)
                for i in range(2):
                    v.sem_inc(s_sent[i], 16)
            else:
                for n in range(NL):
                    v.wait_ge(s_whi, n + 1)
                    v.tensor_tensor(part(1, n), raw[:, n % 2], part(0, n).bitcast(F32), ALU.subtract).then_inc(s_wlo, 1)
            v.wait_ge(s_small, 64)
            for b in range(B):
                if sign:
                    last = v.tensor_scalar(gate[:, :, b], down_scale[:, :], output_scale[:, 0:1], None, ALU.mult)
                else:
                    last = v.tensor_copy(gate[:, :, b], ada[:, GATE2:GATE2 + C, b])
            last.then_inc(s_own, 1)
            v.wait_ge(s_own, 1)
            with v.Fori(0, B) as b:
                v.wait_ge(s_done, b * C + C)
                v.tensor_copy(gate_now[:, :], gate[:, :, bass.ds(b, 1)].rearrange("p c o -> p (c o)")).then_inc(s_own, 1)
                if sign:
                    v.wait_ge(s_xp, 2 * b + 1)
                    v.tensor_tensor(x_p[1][:, :, :], x32[:, :, :], x_p[0][:, :, :].bitcast(F32), ALU.subtract).then_inc(s_xp, 1)
                for j in range(HT):
                    v.wait_ge(s_hhi, b * HT + (j + 1))
                    v.tensor_tensor(h_p[1][:, j % 2, :], h[:, j % 2, :], h_p[0][:, j % 2, :].bitcast(F32), ALU.subtract).then_inc(s_hlo, 1)
                v.wait_ge(s_used, b * HT + (HT + 2))
                v.wait_ge(s_base, 16 * b + 16)
                v.wait_ge(s_own, b + 2)
                for m in range(C):
                    v.scalar_tensor_tensor(out=(final if sign else base)[:, m, :], in0=acc[m][:, :], scalar=gate_now[:, m:m + 1],
                                           in1=base[:, m, :], op0=ALU.mult, op1=ALU.add).then_inc(s_done, 1)
                if sign:
                    for i in range(TT):
                        v.wait_ge(s_tt, b * TT + (i + 1))
                        v.wait_ge(s_sent[i % 2], 32 * b + 16 * (i // 2 + 1))
                        v.tensor_copy(tokens[:, i % 2, :], tb[i % 2][:, :]).then_inc(s_tok, 1)


_INS = ['x', 'cond_2048', 'L0_cond_coupling', 'L0_cond_bias', 'L0_attn_Wqkv_w', 'L0_attn_Wqkv_b', 'L0_cond2_ada_w',
        'L0_cond2_ada_b', 'L0_cond2_qkv_w', 'L0_cond2_qkv_b', 'L0_cond2_out_w', 'L0_cond2_out_b', 'L0_cond2_ffn_w1',
        'L0_cond2_ffn_b1', 'L0_cond2_ffn_w2', 'L0_cond2_ffn_b2', 'L0_ffn_up_weight', 'L0_ffn_down_weight',
        'L0_ffn_up_scale', 'L0_ffn_down_scale', 'L0_ffn_output_scale']


def constants():
    half = DH0 // 2
    inv = (np.float32(1.0) / np.float32(10000.0) ** (np.arange(0, DH0, 2, dtype=np.float32) / np.float32(DH0))).astype(np.float32)
    freqs = np.outer(np.arange(T, dtype=np.float32), inv).astype(np.float32)
    lane = np.arange(P) % DH0
    cos = np.cos(freqs).astype(np.float32).T[lane % half]
    sin = np.sin(freqs).astype(np.float32).T[lane % half] * np.where(lane < half, -1.0, 1.0).astype(np.float32)[:, None]
    swap = np.zeros((P, P), np.float32)
    swap[np.arange(P) ^ half, np.arange(P)] = 1.0
    mask = np.where(np.arange(T)[None, :] > np.arange(P)[:, None], NEG_INF, 0.0).astype(np.float32)
    return {"const_identity": np.eye(P, dtype=np.float32), "const_cos": np.ascontiguousarray(cos),
            "const_sin": np.ascontiguousarray(sin), "const_swap": swap, "const_mask": mask}


def program(nc, io, out):
    def dram(name, dt=F32): return nc.dram_tensor(name, (P, C, B, T), dt, kind="Internal").ap()
    x_dram, trace_dram, xa_dram, x2_dram, x3_base, x3_dram = [dram(n) for n in ("x_t", "trace_t", "xa_t", "x2_t", "x3b_t", "x3_t")]
    n1 = [dram(f"n1_{p}") for p in PARTS]
    n2 = [dram(f"n2_{p}") for p in PARTS]
    cond_dram = nc.dram_tensor("cond_t", (P, C, B), F32, kind="Internal").ap()
    ada_dram = nc.dram_tensor("ada_t", (P, ADA, B), F32, kind="Internal").ap()
    scan_phase(nc, io, x_dram, trace_dram, cond_dram)
    causal_phase(nc, io, x_dram, trace_dram, xa_dram)
    ada_phase(nc, io, cond_dram, ada_dram)
    norm_phase(nc, io, "n_", xa_dram, ada_dram, SHIFT1, SCALE1, GATE1, "L0_cond2_out_b", n1, x2_dram)
    attention_phase(nc, io, n1, ada_dram, x2_dram)
    norm_phase(nc, io, "o_", x2_dram, ada_dram, SHIFT2, SCALE2, GATE2, "L0_cond2_ffn_b2", n2, x3_base)
    ffn_phase(nc, io, False, n2, ada_dram, x3_base, x3_dram)
    ffn_phase(nc, io, True, [x3_dram], None, xa_dram, out)


def kernel(**inputs):
    import concourse.bacc as bacc
    from concourse.bass_utils import run_bass_kernel_spmd
    nc = bacc.Bacc("TRN2", target_bir_lowering=False, num_devices=1)
    arrays, io = {}, {}
    host = {name: np.ascontiguousarray(inputs[name]) for name in _INS}
    host.update(constants())
    for name, a in host.items():
        arrays[name + "_dram"] = a
        io[name] = nc.dram_tensor(name + "_dram", a.shape, mybir.dt.from_np(a.dtype), kind="ExternalInput").ap()
    out = nc.dram_tensor("out_dram", (B, T, D), F32, kind="ExternalOutput").ap()
    program(nc, io, out)
    return run_bass_kernel_spmd(nc, [arrays], core_ids=[0]).results[0]["out_dram"]
```

```python
from contextlib import ExitStack

import numpy as np
import concourse.bass as bass
from concourse import mybir

F32 = mybir.dt.float32
F32R = mybir.dt.float32r
F16 = mybir.dt.float16
ALU = mybir.AluOpType
ACT = mybir.ActivationFunctionType
AX = mybir.AxisListType

P = 128
B, T, D = 4, 512, 512
C = D // P
TOK = B * T
TT = T // P

DT, EPSILON, ALPHA, BETA, CLAMP = 0.01, 0.08, 0.7, 0.8, 20.0
W_SCALE = 64.0
STAGES = 4
START_OF = [0, 0, 1, 2]
HALVES = (slice(0, C // 2), slice(C // 2, C))
STAGE_STEP = [DT / 2, DT / 2, DT, DT / 6]


class Count:

    def __init__(self, sem, start=0):
        self.sem, self.now = sem, start

    def inc(self, ins, by=1):
        ins.then_inc(self.sem, by)
        self.now += by
        return self.now


def scan_phase(nc, io, x_dram, trace_dram, cond_dram):
    sems = []
    with ExitStack() as ctx:
        def sb(n, s, d): return ctx.enter_context(nc.sbuf_tensor(n, s, d))
        def ps(n): return ctx.enter_context(nc.psum_tensor(n, [P, 512], F32))
        def sem(n):
            sems.append(nc.alloc_semaphore(n))
            return sems[-1]
        xT = sb("xT", [P, C, B, T], F32)
        condT = sb("condT", [P, C, B], F32)
        identity = sb("identity", [P, P], F32)
        rows = sb("rows", [P, 4, D], F32)
        coup = sb("coup", [P, C, D], F32)
        cond_rows = sb("cond_rows", [B, D], F32)
        wT = sb("wT", [P, C, D], F32)
        w_hi = sb("w_hi", [P, C, D], F16)
        w_lo = sb("w_lo", [P, C, D], F16)
        bias_c = sb("bias_c", [P, C], F32)
        bias = sb("bias", [P, C, B], F32)
        trace = sb("trace", [P, C, B, T + 1], F32)
        tanh_parts = sb("tanh_parts", [P, 2, C, 2, B], F16)
        tanh_full = sb("tanh_full", [P, 2, C, B], F32)
        scratch = sb("scratch", [P, 8], F32)
        q_new = sb("q_new", [P, C, B], F32)
        q = sb("q", [P, STAGES, C, B], F32)
        pst = sb("pst", [P, STAGES, C, B], F32)
        p_new = sb("p_new", [P, C, B], F32)
        drive = sb("drive", [P, C, B], F32)
        rate = sb("rate", [P, STAGES, C, B], F32)
        z_sum = sb("z_sum", [P, C, B], F32)
        pz_sum = sb("pz_sum", [P, C, B], F32)
        start_p = sb("start_p", [P, STAGES, C, B], F32)
        start_q = sb("start_q", [P, C, B], F32)
        start = sb("start", [P, 3, C, B], F32)
        p_alpha = sb("p_alpha", [P, 2, C, B], F32)
        cub = sb("cub", [P, C, B], F32)
        slope = sb("slope", [P, C, B], F32)
        local = sb("local", [P, C, B], F32)
        base = sb("base", [P, C, B], F32)
        base_lo = sb("base_lo", [P, C, B], F32)
        gp = sb("gp", [P, 11, C, B], F32)
        consts = sb("consts", [P, 10, C, B], F32)
        banks = [ps(f"bank{i}") for i in range(4)]
        s_rows = [sem(f"s_rows{i}") for i in range(2)]
        s_coup, s_small, s_tr, s_ev, s_w, s_pre = [sem("s_" + n) for n in ("coup", "small", "tr", "ev", "w", "pre")]
        s_q = sem("s_q")
        s_clip = sem("s_clip")
        s_th = sem("s_th")
        s_tf = sem("s_tf")
        s_tl = sem("s_tl")
        s_mm = sem("s_mm")
        s_rate = sem("s_rate")
        s_start = sem("s_start")
        s_drive = sem("s_drive")
        s_z = sem("s_z")
        s_pz = sem("s_pz")
        s_palpha = sem("s_palpha")
        s_pclip = sem("s_pclip")
        s_dve, s_pool = sem("s_dve"), sem("s_pool")
        s_trace = sem("s_trace")
        s_table, s_out = sem("s_table"), sem("s_out")
        block = ctx.enter_context(nc.Block())

        x_tiles = io["x"].rearrange("b (i r p) d -> (b i) p r d", p=P, r=2)
        PAIRS = B * TT // 2

        @block.sync
        def _(sp):
            sp.dma_start(coup[:, :, :], io["L0_cond_coupling"].rearrange("(c p) k -> p c k", p=P)).then_inc(s_coup, 16)
            for j in range(PAIRS):
                if j >= 2:
                    sp.wait_ge(s_tr, C + 2 * (j - 1))
                sp.dma_start(rows[:, 2 * (j % 2):2 * (j % 2) + 2, :], x_tiles[j]).then_inc(s_rows[j % 2], 16)
            sp.wait_ge(s_ev, C + 2 * PAIRS)
            sp.dma_start(x_dram, xT[:, :, :, :]).then_inc(s_out, 16)
            sp.wait_ge(s_w, 3)
            sp.dma_start(cond_dram, condT[:, :, :]).then_inc(s_out, 16)
            sp.wait_ge(s_trace, 1)
            sp.dma_start(trace_dram, trace[:, :, :, 1:T + 1]).then_inc(s_out, 16)
            sp.wait_ge(s_out, 48)

        @block.scalar
        def _(act):
            act.dma_start(identity[:, :], io["const_identity"]).then_inc(s_small, 16)
            act.dma_start(cond_rows[:, :], io["cond_2048"]).then_inc(s_small, 16)
            with nc.allow_non_contiguous_dma(reason="512 bias values, once"):
                act.dma_start(bias_c[:, :], io["L0_cond_bias"].rearrange("(c p) -> p c", p=P)).then_inc(s_small, 16)
            act.wait_ge(s_pre, 1)
            act.activation(scratch[:, 4:8], scratch[:, 0:4], ACT.Tanh).then_inc(s_table, 1)
            with act.Fori(0, T) as t:
                for s in range(STAGES):
                    u = s % 2
                    src = q_new if s == 0 else q[:, s]
                    for half, at in enumerate(HALVES):
                        act.wait_ge(s_q, t * 2 * STAGES + (2 * s + half + 1))
                        act.activation(tanh_parts[:, u, at, 0, :], src[:, at, :], ACT.Tanh).then_inc(s_th, 1)
                        act.activation(tanh_full[:, u, at], src[:, at, :], ACT.Tanh).then_inc(s_tf, 1)

        @block.tensor
        def _(pe):
            pe.wait_ge(s_small, 48)
            pe.wait_ge(s_coup, 16)
            for k in range(C):
                for m in range(C):
                    last = pe.matmul(banks[k][:, m * P:(m + 1) * P], coup[:, m, k * P:(k + 1) * P], identity[:, :],
                                     start=(m == 0), stop=(m == C - 1), skip_group_check=True)
                last.then_inc(s_tr, 1)
            for j in range(2 * PAIRS):
                if j % 2 == 0:
                    pe.wait_ge(s_rows[(j // 2) % 2], 16 * (j // 4 + 1))
                pe.wait_ge(s_ev, j + 1)
                for c in range(C):
                    last = pe.matmul(banks[j % 4][:, c * P:(c + 1) * P], rows[:, j % 4, c * P:(c + 1) * P], identity[:, :],
                                     start=(c == 0), stop=(c == C - 1), skip_group_check=True)
                last.then_inc(s_tr, 1)
            pe.wait_ge(s_ev, 2 * PAIRS + 1)
            for c in range(C):
                last = pe.matmul(banks[0][:, c * B:(c + 1) * B], cond_rows[:, c * P:(c + 1) * P], identity[0:B, 0:B],
                                 start=(c == 0), stop=(c == C - 1), skip_group_check=True)
            last.then_inc(s_tr, 1)
            pe.wait_ge(s_w, 3)
            with pe.Fori(0, T) as t:
                for s in range(STAGES):
                    u = s % 2
                    out = banks[2 * u:2 * u + 2]

                    def block_product(w, m, k, parts, **flags):
                        at = (m % 2) * 2 * B
                        return pe.matmul(out[m // 2][:, at:at + parts * B], w[:, k, m * P:(m + 1) * P], tanh_parts[:, u, k, 0:parts, :],
                                         skip_group_check=True, **flags)

                    def blocks(w, outputs, inputs, parts):
                        for m in outputs:
                            for k in inputs:
                                last = block_product(w, m, k, parts, start=(w is w_lo and m % 2 == 0 and k == 0),
                                                     stop=(w is w_hi and m % 2 == 1 and k == C - 1))
                        return last

                    pe.wait_ge(s_th, t * 2 * STAGES + (2 * s + 1))
                    blocks(w_lo, (0, 1, 2, 3), (0, 1), 1)
                    pe.wait_ge(s_th, t * 2 * STAGES + (2 * s + 2))
                    blocks(w_lo, (0, 1, 2, 3), (2, 3), 1)
                    pe.wait_ge(s_tl, t * 2 * STAGES + (2 * s + 1))
                    blocks(w_hi, (0, 1), (0, 1), 2)
                    pe.wait_ge(s_tl, t * 2 * STAGES + (2 * s + 2))
                    blocks(w_hi, (0, 1), (2, 3), 2).then_inc(s_mm, 1)
                    blocks(w_hi, (2, 3), (0, 1, 2, 3), 2).then_inc(s_mm, 1)

        @block.vector
        def _(v):
            v.memset(scratch[:, 0:4], 0.0).then_inc(s_pre, 1)
            for k in range(C):
                v.wait_ge(s_tr, k + 1)
                v.tensor_scalar(wT[:, k, :], banks[k][:, :], W_SCALE, None, ALU.mult).then_inc(s_ev, 1)
            v.wait_ge(s_ev, C)
            v.tensor_copy(w_hi[:, :, :], wT[:, :, :]).then_inc(s_w, 1)
            v.wait_ge(s_w, 1)
            v.tensor_tensor(w_lo[:, :, :], wT[:, :, :], w_hi[:, :, :], ALU.subtract).then_inc(s_w, 1)
            for j in range(2 * PAIRS):
                b, i = j // TT, j % TT
                v.wait_ge(s_tr, C + j + 1)
                v.tensor_copy(xT[:, :, b, i * P:(i + 1) * P], banks[j % 4][:, :].rearrange("p (c t) -> p c t", c=C)).then_inc(s_ev, 1)
            v.wait_ge(s_tr, C + 2 * PAIRS + 1)
            condv = banks[0][:, 0:C * B].rearrange("p (c b) -> p c b", c=C)
            v.tensor_copy(condT[:, :, :], condv).then_inc(s_w, 1)
            v.tensor_copy(pst[:, 0], condv).then_inc(s_pclip, 1)
            v.tensor_copy(q[:, 0], condv).then_inc(s_clip, 1)
            v.tensor_copy(q_new[:, :, :], condv).then_inc(s_q, 2)
            v.wait_ge(s_q, 2)
            with v.Fori(0, T) as t:
                n = 0

                def own(ins):
                    nonlocal n
                    ins.then_inc(s_dve, 1)
                    n += 1
                    return n

                def stt(out, in0, scalar, in1, op0=ALU.mult, op1=ALU.add):
                    return v.scalar_tensor_tensor(out=out, in0=in0, scalar=scalar, in1=in1, op0=op0, op1=op1)

                def after(mark):
                    v.wait_ge(s_dve, mark)

                v.sem_clear(s_dve)
                for s in range(STAGES):
                    u = s % 2
                    a = STAGE_STEP[s]

                    def low_part(half):
                        at = HALVES[half]
                        v.wait_ge(s_tf, t * 2 * STAGES + (2 * s + half + 1))
                        v.tensor_tensor(tanh_parts[:, u, at, 1, :], tanh_full[:, u, at], tanh_parts[:, u, at, 0, :],
                                        ALU.subtract).then_inc(s_tl, 1)

                    if s == 0:
                        v.wait_ge(s_clip, t + 1)
                    else:
                        v.wait_ge(s_q, t * 2 * STAGES + (2 * s + 2))
                    cubed = own(stt(cub[:, :, :], q[:, s], -1.0 / 3.0, q[:, s], ALU.mult, ALU.mult))
                    if s == 0:
                        v.wait_ge(s_pclip, t + 1)
                    stt(rate[:, s], pst[:, s], -BETA, q[:, s]).then_inc(s_rate, 1)
                    if s == 0:
                        v.wait_ge(s_drive, t + 1)
                        begun = own(stt(start[:, 0], drive[:, :, :], DT / 2, q[:, 0]))
                        low_part(0)
                    after(cubed)
                    sloped = own(stt(slope[:, :, :], cub[:, :, :], 1.0, q[:, s], ALU.add, ALU.mult))
                    if s == 0:
                        after(begun)
                        shifted = own(stt(start_p[:, 0], pst[:, 0], -DT / 2, start[:, 0]))
                    if s > 0:
                        low_part(0)
                    low_part(1)
                    if s == 0:
                        own(stt(start[:, 1], drive[:, :, :], DT, q[:, 0]))
                        stt(start[:, 2], drive[:, :, :], DT / 6, q[:, 0]).then_inc(s_start, 1)
                        v.wait_ge(s_palpha, t + 1)
                    if s < 3:
                        v.wait_ge(s_rate, t * STAGES + (s + 1))
                        moved = own(stt(pst[:, s + 1], rate[:, s], EPSILON * a, p_alpha[:, START_OF[s]]))
                    else:
                        v.wait_ge(s_z, t + 1)
                        shifted = own(stt(start_p[:, 3], pst[:, 3], -DT / 6, z_sum[:, :, :]))
                        after(sloped)
                        v.wait_ge(s_pz, t + 1)
                        moved = own(stt(p_new[:, :, :], rate[:, 3], EPSILON * DT / 6, pz_sum[:, :, :]))
                        after(shifted)
                        shifted = own(stt(start_q[:, :, :], q[:, 3], 1.0 / 3.0, start_p[:, 3]))
                    after(max(shifted, sloped) if s in (0, 3) else sloped)
                    based = own(stt(base[:, :, :], slope[:, :, :], a, start_q[:, :, :] if s == 3 else start_p[:, s]))
                    if s < 2:
                        after(moved)
                        shifted = own(stt(start_p[:, s + 1], pst[:, s + 1], -STAGE_STEP[s + 1], start[:, START_OF[s + 1]]))
                    if s == 3:
                        after(moved)
                        v.tensor_scalar(pst[:, 0], p_new[:, :, :], -CLAMP, CLAMP, ALU.max, ALU.min).then_inc(s_pclip, 1)
                    sums = [banks[2 * u + half][:, 0:C * B].rearrange("p (c h b) -> p c h b", c=2, h=2) for half in range(2)]
                    dst = q[:, s + 1] if s < 3 else q_new
                    after(based)
                    lows = []
                    for half, at in enumerate(HALVES):
                        v.wait_ge(s_mm, t * 2 * STAGES + (2 * s + half + 1))
                        lows.append(own(stt(base_lo[:, at, :], sums[half][:, :, 1, :], a / W_SCALE, base[:, at, :])))
                    for half, at in enumerate(HALVES):
                        after(lows[half])
                        stt(dst[:, at, :], sums[half][:, :, 0, :], a / W_SCALE, base_lo[:, at, :]).then_inc(s_q, 1)
                v.wait_ge(s_q, t * 2 * STAGES + (2 * STAGES + 2))
                v.tensor_scalar(q[:, 0], q_new[:, :, :], -CLAMP, CLAMP, ALU.max, ALU.min).then_inc(s_clip, 1)

        @block.gpsimd
        def _(g):
            g.wait_ge(s_small, 48)
            for b in range(B):
                last = g.tensor_copy(bias[:, :, b], bias_c[:, :])
            values = [1.0 / 3.0, 2.0 / 3.0, EPSILON * DT / 6.0, 6 * ALPHA] + [EPSILON * ALPHA * a for a in (DT / 2, DT)]
            c_third, c_two_thirds, c_psum, c_6alpha, c_ahalf, c_afull = [consts[:, i] for i in range(len(values))]
            for i, value in enumerate(values):
                last = g.memset(consts[:, i], value)
            last.then_inc(s_pool, 1)
            g.wait_ge(s_ev, C + 2 * PAIRS)
            g.wait_ge(s_pool, 1)
            with g.Fori(0, T) as t:
                n = 0

                def own(ins):
                    nonlocal n
                    ins.then_inc(s_pool, 1)
                    n += 1
                    return n

                def tt(out, a, b, op=ALU.add):
                    return g.tensor_tensor(out, a, b, op)

                def after(mark):
                    g.wait_ge(s_pool, mark)

                g.sem_clear(s_pool)
                tt(drive[:, :, :], xT[:, :, :, bass.ds(t, 1)].rearrange("p c b o -> p c (b o)"), bias[:, :, :]).then_inc(s_drive, 1)
                g.wait_ge(s_pclip, t + 1)
                tt(p_alpha[:, 0], pst[:, 0], c_ahalf)
                tt(p_alpha[:, 1], pst[:, 0], c_afull).then_inc(s_palpha, 1)
                g.wait_ge(s_clip, t + 1)
                g.tensor_copy(trace[:, :, :, bass.ds(t, 1)].rearrange("p c b o -> p c (b o)"), q[:, 0])
                g.wait_ge(s_rate, t * STAGES + 1)
                r0 = own(tt(gp[:, 0], rate[:, 0], c_6alpha))
                g.wait_ge(s_q, t * 2 * STAGES + 4)
                d1 = own(tt(gp[:, 1], q[:, 1], q[:, 0], ALU.subtract))
                after(d1)
                m1 = own(tt(gp[:, 2], gp[:, 1], q[:, 0], ALU.subtract))
                after(m1)
                m2 = own(tt(gp[:, 5], gp[:, 2], c_third, ALU.mult))
                g.wait_ge(s_start, t + 1)
                after(m2)
                z1 = own(tt(gp[:, 7], gp[:, 5], start[:, 2]))
                g.wait_ge(s_q, t * 2 * STAGES + 6)
                d2 = own(tt(gp[:, 3], q[:, 2], q[:, 0], ALU.subtract))
                g.wait_ge(s_rate, t * STAGES + 3)
                r12 = own(tt(gp[:, 4], rate[:, 1], rate[:, 2]))
                after(d2)
                z2 = own(tt(gp[:, 9], gp[:, 3], c_two_thirds, ALU.mult))
                after(r12)
                p1 = own(tt(gp[:, 6], gp[:, 4], gp[:, 4]))
                after(max(z1, z2))
                tt(z_sum[:, :, :], gp[:, 7], gp[:, 9]).then_inc(s_z, 1)
                after(p1)
                p2 = own(tt(gp[:, 8], gp[:, 6], gp[:, 0]))
                after(p2)
                p3 = own(tt(gp[:, 10], gp[:, 8], c_psum, ALU.mult))
                after(p3)
                tt(pz_sum[:, :, :], gp[:, 10], pst[:, 0]).then_inc(s_pz, 1)
            g.wait_ge(s_clip, T + 1)
            g.tensor_copy(trace[:, :, :, T], q[:, 0]).then_inc(s_trace, 1)
    nc.clear_and_free_semaphores(sems)
    nc.all_engine_barrier()



class Attention:

    def __init__(self, nc, ctx, heads, scale, masked, turned_banks):
        def sb(n, s, d): return ctx.enter_context(nc.sbuf_tensor(n, s, d))
        def ps(n): return ctx.enter_context(nc.psum_tensor(n, [P, 512], F32))
        def sem(n): return ctx.enter_context(nc.semaphore(n))
        name = "m" if masked else "f"
        self.heads, self.scale, self.masked = heads, scale, masked
        self.probs = sb(name + "_probs", [P, 2, TT, T], F32)
        self.pt = [sb(name + f"_pt_{part}", [P, TT, TT, P], F32R) for part in ("hi", "lo")]
        self.diag = sb(name + "_diag", [P, TT, P], F32)
        self.peak = sb(name + "_peak", [P, TT], F32)
        self.shift = sb(name + "_shift", [P, TT], F32)
        self.sums = sb(name + "_sums", [P, TT], F32)
        self.inverse = sb(name + "_inverse", [P, TT], F32)
        self.s_bank = [ps(name + f"_scores{i}") for i in range(2)]
        self.t_bank = [ps(name + f"_turned{i}") for i in range(max(turned_banks) + 1)]
        self.t_of = turned_banks
        self.t_age = [next(n for n in range(1, TT + 1) if turned_banks[(i - n) % TT] == turned_banks[i]) for i in range(TT)]
        self.o_bank = ps(name + "_out")
        self.scored = sem(name + "_scored")
        self.peaked = sem(name + "_peaked")
        self.exped = sem(name + "_exped")
        self.scaled = sem(name + "_scaled")
        self.turned = sem(name + "_turned")
        self.high = sem(name + "_high")
        self.low = sem(name + "_low")
        self.valued = sem(name + "_valued")
        self.own = sem(name + "_own")
        self.taken = sem(name + "_taken")

    def start_act(self, act):
        act.sem_inc(self.exped, 2)

    def start_dve(self, v):
        v.sem_inc(self.low, TT)

    def start_pe(self, pe):
        pe.sem_inc(self.valued, 1)
        pe.sem_inc(self.turned, TT)


    def pe_scores(self, pe, unit, i, q, k, extra=None):
        out = self.s_bank[i % 2]
        pe.wait_ge(self.exped, unit * TT + (i + 1))
        pairs = [(0, 0), (0, 1), (1, 0)]
        for n, (a, b) in enumerate(pairs):
            last = pe.matmul(out[:, :], q[a][:, i * P:(i + 1) * P], k[b], start=(n == 0),
                             stop=(n == 2 and extra is None), skip_group_check=True)
        if extra is not None:
            last = pe.matmul(out[:, i * P:T], extra[0], extra[1][:, 0:T - i * P], start=False, stop=True, skip_group_check=True)
        last.then_inc(self.scored, 1)

    def pe_turn(self, pe, unit, i, parity):
        if i == 0:
            pe.wait_ge(self.scaled, unit + 1)
        pe.wait_ge(self.low, unit * TT + (TT + i + 1 - self.t_age[i]))
        out = self.t_bank[self.t_of[i]]
        for j in range(TT):
            last = pe.matmul(out[:, j * P:(j + 1) * P], self.probs[:, parity, i, j * P:(j + 1) * P], self.diag[:, i, :],
                             start=(j == 0), stop=(j == TT - 1), skip_group_check=True)
        last.then_inc(self.turned, 1)

    def pe_values(self, pe, unit, v):
        pe.wait_ge(self.low, unit * TT + 2 * TT)
        pe.wait_ge(self.taken, unit + 1)
        n = 0
        for j in range(TT):
            for a, b in ((0, 0), (0, 1), (1, 0)):
                last = pe.matmul(self.o_bank[:, :], v(a, j), self.pt[b][:, :, j, :], start=(n == 0), stop=(n == 3 * TT - 1))
                n += 1
        last.then_inc(self.valued, 1)

    def act_exp(self, act, unit, i, parity):
        act.wait_ge(self.peaked, unit * TT + (i + 1))
        act.activation(self.probs[:, parity, i, :], self.s_bank[i % 2][:, :], ACT.Exp, bias=self.shift[:, i:i + 1],
                       scale=self.scale, accum_out=self.sums[:, i:i + 1]).then_inc(self.exped, 1)

    def act_high(self, act, unit, i):
        act.wait_ge(self.turned, unit * TT + (TT + i + 1))
        if i == 0:
            act.wait_ge(self.valued, unit + 1)
        act.activation(self.pt[0][:, i], self.t_bank[self.t_of[i]][:, :].rearrange("p (j t) -> p j t", j=TT), ACT.Copy).then_inc(self.high, 1)

    def dve_peak(self, v, unit, i):
        v.wait_ge(self.scored, unit * TT + (i + 1))
        if self.scale == 1.0:
            v.reduce_max(self.shift[:, i:i + 1], self.s_bank[i % 2][:, :], AX.X, negate=True).then_inc(self.peaked, 1)
            return
        v.reduce_max(self.peak[:, i:i + 1], self.s_bank[i % 2][:, :], AX.X).then_inc(self.own, 1)
        v.wait_ge(self.own, unit * (TT + 1) + (i + 1))
        v.tensor_scalar(self.shift[:, i:i + 1], self.peak[:, i:i + 1], -self.scale, None, ALU.mult).then_inc(self.peaked, 1)

    def dve_scale(self, v, unit, identity):
        v.wait_ge(self.exped, unit * TT + (TT + 2))
        v.reciprocal(self.inverse[:, :], self.sums[:, :]).then_inc(self.own, 1)
        v.wait_ge(self.turned, unit * TT + TT)
        per_unit = 1 if self.scale == 1.0 else TT + 1
        v.wait_ge(self.own, unit * per_unit + per_unit)
        for i in range(TT):
            last = v.tensor_scalar(self.diag[:, i, :], identity, self.inverse[:, i:i + 1], None, ALU.mult)
        last.then_inc(self.scaled, 1)

    def dve_low(self, v, unit, i):
        v.wait_ge(self.high, unit * TT + (i + 1))
        v.tensor_tensor(self.pt[1][:, i], self.t_bank[self.t_of[i]][:, :].rearrange("p (j t) -> p j t", j=TT),
                        self.pt[0][:, i].bitcast(F32), ALU.subtract).then_inc(self.low, 1)


def pipeline(heads, scores, turn, values, fill=lambda slot: None):
    for u in range(heads + 2):
        if u < heads:
            scores(u, 0)
            scores(u, 1)
        fill((u, "middle"))
        if u >= 2:
            values(u - 2)
        if u < heads:
            scores(u, 2)
            scores(u, 3)
        for i in range(TT):
            if 0 <= u - 1 < heads:
                turn(u - 1, i)
        fill((u, "end"))


PARTS = (0, 1)
PRODUCTS = ((0, 0), (0, 1), (1, 0))


def product(pe, out, weight, activation, chunks):
    n = 0
    for k in range(chunks):
        for a, b in PRODUCTS:
            last = pe.matmul(out, weight(a, k), activation(b, k), start=(n == 0), stop=(n == 3 * chunks - 1))
            n += 1
    return last


H0, DH0 = 16, 32
M0 = D // P
NEG_INF = -10000.0


def causal_phase(nc, io, x_dram, trace_dram, xa_dram):
    with ExitStack() as ctx:
        def sb(n, s, d=F32): return ctx.enter_context(nc.sbuf_tensor(n, s, d))
        def sem(n): return ctx.enter_context(nc.semaphore(n))
        core = Attention(nc, ctx, H0, 1.0, True, (0, 1, 2, 3))
        banks = core.t_bank[2:4] + [ctx.enter_context(nc.psum_tensor("swapped", [P, 512], F32))]
        identity = sb("ident2", [P, P])
        identity_r = sb("identity_r", [P, P], F32R)
        swap_r = sb("swap_r", [P, P], F32R)
        mask_r = sb("mask_r", [P, T], F32R)
        cos, sin = sb("cos", [P, T]), sb("sin", [P, T])
        qk_bias = sb("qk_bias", [P, 2 * M0])
        v_bias = sb("v_bias", [P, D])
        rows = sb("w_rows", [P, 2, D])
        wT = [sb(f"wT_{p}", [P, C, 3 * D], F32R) for p in ("hi", "lo")]
        tr = sb("tr", [P, C, T])
        tr_p = [sb(f"tr_{p}", [P, C, T], F32R) for p in ("hi", "lo")]
        xb = sb("xb", [P, C, T])
        u = sb("u", [P, 2, T])
        u_p = [sb(f"u_{p}", [P, 2, T], F32R) for p in ("hi", "lo")]
        turn_a, turn_b, turned, vf = [core.probs[:, i // 2, 2 * (i % 2):2 * (i % 2) + 2, :] for i in range(4)]
        qk = [sb(f"qk_{p}", [P, 2 * M0, T], F32R) for p in ("hi", "lo")]
        q_alone = [sb(f"q_alone_{p}", [P, 4, T], F32R) for p in ("hi", "lo")]
        zeros = sb("zeros", [P, T])
        val = [sb(f"val_{p}", [P, TT, D], F32R) for p in ("hi", "lo")]
        s_const, s_w, s_cast, s_tr = sem("c_const"), [sem("c_w0"), sem("c_w1")], sem("c_cast"), sem("c_tr")
        s_wev, s_whi = sem("c_wev"), sem("c_whi")
        s_in = sem("c_in")
        s_split = sem("c_split")
        s_ahi = sem("c_ahi")
        s_proj = sem("c_proj")
        s_u = sem("c_u")
        s_uhi = sem("c_uhi")
        s_ulo = sem("c_ulo")
        s_swap = sem("c_swap")
        s_rot = sem("c_rot")
        s_rhi = sem("c_rhi")
        s_rlo = sem("c_rlo")
        s_vf, s_vhi, s_vlo = sem("c_vf"), sem("c_vhi"), sem("c_vlo")
        s_zero, s_alone = sem("c_zero"), sem("c_alone")
        s_own = sem("c_own")
        s_out = sem("c_out")
        block = ctx.enter_context(nc.Block())
        w_tiles = io["L0_attn_Wqkv_w"].rearrange("(m p) k -> m p k", p=P)
        MT = 3 * D // P
        QK = 2 * M0
        LOADS = 7

        @block.sync
        def _(sp):
            for m in range(MT):
                if m >= 2:
                    sp.wait_ge(s_tr, m - 1)
                sp.dma_start(rows[:, m % 2, :], w_tiles[m]).then_inc(s_w[m % 2], 16)
            with sp.Fori(0, B) as b:
                sp.wait_ge(s_out, 16 * b + 16)
                sp.dma_start(tr[:, :, :], trace_dram[:, :, bass.ds(b, 1), :].rearrange("p c o t -> p c (o t)")).then_inc(s_in, 16)
                sp.dma_start(xb[:, :, :], x_dram[:, :, bass.ds(b, 1), :].rearrange("p c o t -> p c (o t)")).then_inc(s_in, 16)
                sp.wait_ge(core.taken, b * H0 + (H0 + 1))
                sp.dma_start(xa_dram[:, :, bass.ds(b, 1), :].rearrange("p c o t -> p c (o t)"), xb[:, :, :]).then_inc(s_out, 16)
            sp.wait_ge(s_out, 16 * B + 16)

        @block.gpsimd
        def _(g):
            g.dma_start(identity[:, :], io["const_identity"]).then_inc(s_const, 16)
            g.dma_start(identity_r[:, :], io["const_identity"]).then_inc(s_const, 16)
            g.dma_start(swap_r[:, :], io["const_swap"]).then_inc(s_const, 16)
            g.dma_start(mask_r[:, :], io["const_mask"]).then_inc(s_const, 16)
            g.dma_start(cos[:, :], io["const_cos"]).then_inc(s_const, 16)
            g.dma_start(sin[:, :], io["const_sin"]).then_inc(s_const, 16)
            with nc.allow_non_contiguous_dma(reason="1024 bias values, once"):
                g.dma_start(qk_bias[:, :], io["L0_attn_Wqkv_b"][0:2 * D].rearrange("(m p) -> p m", p=P)).then_inc(s_const, 16)
            g.dma_start(v_bias[:, :], io["L0_attn_Wqkv_b"][2 * D:3 * D].partition_broadcast(P)).then_inc(s_const, 16)
            g.memset(zeros[:, :], 0.0).then_inc(s_zero, 1)
            g.wait_ge(s_zero, 1)
            for n in range(4):
                for p in PARTS:
                    last = g.tensor_copy(q_alone[p][:, n, :], zeros[:, :])
            last.then_inc(s_zero, 1)
            g.wait_ge(s_zero, 2)
            with g.Fori(0, B) as b:
                g.wait_ge(s_rlo, b * QK + QK)
                for h in range(H0):
                    rows_of, m = slice(DH0 * (h % 4), DH0 * (h % 4) + DH0), h // 4
                    if h >= 4:
                        g.wait_ge(core.scored, b * H0 * TT + (h - 3) * TT)
                    for p in PARTS:
                        last = g.tensor_tensor(q_alone[p][rows_of, h % 4, :], qk[p][rows_of, m, :].bitcast(F32), zeros[rows_of, :], ALU.add)
                    last.then_inc(s_alone, 1)

        @block.tensor
        def _(pe):
            core.start_pe(pe)
            pe.wait_ge(s_const, 128)
            for m in range(MT):
                pe.wait_ge(s_w[m % 2], 16 * (m // 2 + 1))
                if m >= 2:
                    pe.wait_ge(s_wev, m - 1)
                for k in range(C):
                    last = pe.matmul(banks[m % 2][:, k * P:(k + 1) * P], rows[:, m % 2, k * P:(k + 1) * P], identity[:, :],
                                     start=(k == 0), stop=(k == C - 1), skip_group_check=True)
                last.then_inc(s_tr, 1)
            pe.wait_ge(s_wev, MT)
            with pe.Fori(0, B) as b:
                pe.wait_ge(s_ahi, b + 1)
                pe.wait_ge(s_split, b + 1)

                def project(m):
                    pe.wait_ge(s_u, b * QK + (m + 1))
                    product(pe, banks[m % 2][:, :], lambda a, k: wT[a][:, k, m * P:(m + 1) * P],
                            lambda a, k: tr_p[a][:, k, :], C).then_inc(s_proj, 1)

                def swapped(m):
                    pe.wait_ge(s_ulo, b * QK + (m + 1))
                    pe.wait_ge(s_rot, b * QK + (m + 1))
                    pe.matmul(banks[2][:, :], swap_r[:, :], u_p[0][:, m % 2, :], start=True, stop=False)
                    pe.matmul(banks[2][:, :], swap_r[:, :], u_p[1][:, m % 2, :], start=False, stop=True).then_inc(s_swap, 1)

                project(0)
                for m in range(1, QK):
                    project(m)
                    swapped(m - 1)
                for i in range(TT):
                    if i < 2:
                        pe.wait_ge(s_u, b * QK + (QK + i + 1))
                    else:
                        pe.wait_ge(s_vf, b * TT + (i - 1))
                    n = 0
                    for k in range(C):
                        for a, c in PRODUCTS:
                            last = pe.matmul(banks[i % 2][:, :], tr_p[a][:, k, i * P:(i + 1) * P], wT[c][:, k, 2 * D:3 * D],
                                             start=(n == 0), stop=(n == 3 * C - 1))
                            n += 1
                    last.then_inc(s_proj, 1)
                    if i == 0:
                        swapped(QK - 1)
                pe.wait_ge(s_rlo, b * QK + QK)
                pe.wait_ge(s_vlo, b * TT + TT)

                def scores(h, i):
                    m = h // 4
                    if i == 0:
                        pe.wait_ge(s_alone, b * H0 + (h + 1))
                    core.pe_scores(pe, b * H0 + h, i, [q_alone[a][:, h % 4, :] for a in PARTS],
                                   [qk[a][:, M0 + m, :] for a in PARTS], extra=(identity_r[:, :], mask_r))

                pipeline(H0, scores, lambda h, i: core.pe_turn(pe, b * H0 + h, i, h % 2),
                         lambda h: core.pe_values(pe, b * H0 + h, lambda a, j: val[a][:, j, (h // 4) * P:(h // 4 + 1) * P]))

        @block.scalar
        def _(act):
            core.start_act(act)
            for m in range(MT):
                act.wait_ge(s_tr, m + 1)
                act.activation(wT[0][:, :, m * P:(m + 1) * P], banks[m % 2][:, :].rearrange("p (k o) -> p k o", k=C),
                               ACT.Copy).then_inc(s_whi, 1)
            act.sem_inc(s_u, 2)
            act.wait_ge(s_const, 128)
            with act.Fori(0, B) as b:
                act.wait_ge(s_in, 32 * b + 32)
                act.activation(tr_p[0][:, :, :], tr[:, :, :], ACT.Copy).then_inc(s_ahi, 1)

                def rotated_high(m):
                    act.wait_ge(s_rot, b * QK + (m + 2))
                    act.activation(qk[0][:, m, :], turned[:, m % 2, :], ACT.Copy).then_inc(s_rhi, 1)

                for m in range(QK):
                    act.wait_ge(s_proj, b * (QK + TT) + (m + 1))
                    act.activation(u[:, m % 2, :], banks[m % 2][:, :], ACT.Identity, bias=qk_bias[:, m:m + 1]).then_inc(s_u, 1)
                    act.wait_ge(s_u, b * QK + (m + 3))
                    act.wait_ge(s_swap, b * QK + (m - 1 + 2))
                    act.activation(u_p[0][:, m % 2, :], u[:, m % 2, :], ACT.Copy).then_inc(s_uhi, 1)
                    if m >= 1:
                        rotated_high(m - 1)
                rotated_high(QK - 1)
                for i in range(TT):
                    act.wait_ge(s_vf, b * TT + (i + 1))
                    act.activation(val[0][:, i, :], vf[:, i % 2, :], ACT.Copy).then_inc(s_vhi, 1)
                pipeline(H0, lambda h, i: core.act_exp(act, b * H0 + h, i, h % 2),
                         lambda h, i: core.act_high(act, b * H0 + h, i), lambda h: None)

        @block.vector
        def _(v):
            core.start_dve(v)
            v.sem_inc(core.taken, 1)
            v.sem_inc(s_rot, 1)
            v.sem_inc(s_out, 16)
            v.sem_inc(s_swap, 2)
            for m in range(MT):
                v.wait_ge(s_whi, m + 1)
                v.tensor_tensor(wT[1][:, :, m * P:(m + 1) * P], banks[m % 2][:, :].rearrange("p (k o) -> p k o", k=C),
                                wT[0][:, :, m * P:(m + 1) * P].bitcast(F32), ALU.subtract).then_inc(s_wev, 1)
            v.wait_ge(s_const, 128)
            with v.Fori(0, B) as b:
                v.wait_ge(s_ahi, b + 1)
                v.tensor_tensor(tr_p[1][:, :, :], tr[:, :, :], tr_p[0][:, :, :].bitcast(F32), ALU.subtract).then_inc(s_split, 1)
                scale = float(1.0 / np.sqrt(DH0))
                for m in range(QK):
                    w = m % 2
                    f = 1.0 if m < M0 else scale
                    v.wait_ge(s_uhi, b * QK + (m + 1))
                    v.tensor_tensor(u_p[1][:, w, :], u[:, w, :], u_p[0][:, w, :].bitcast(F32), ALU.subtract).then_inc(s_ulo, 1)
                    v.scalar_tensor_tensor(out=turn_a[:, w, :], in0=u[:, w, :], scalar=f, in1=cos[:, :], op0=ALU.mult, op1=ALU.mult)\
                        .then_inc(s_own, 1)
                    v.wait_ge(s_swap, b * QK + (m + 3))
                    v.scalar_tensor_tensor(out=turn_b[:, w, :], in0=banks[2][:, :], scalar=f, in1=sin[:, :], op0=ALU.mult, op1=ALU.mult)\
                        .then_inc(s_own, 1)
                    v.wait_ge(s_own, b * 2 * QK + (2 * m + 2))
                    v.tensor_tensor(turned[:, w, :], turn_a[:, w, :], turn_b[:, w, :], ALU.add).then_inc(s_rot, 1)
                    v.wait_ge(s_rhi, b * QK + (m + 1))
                    v.tensor_tensor(qk[1][:, m, :], turned[:, w, :], qk[0][:, m, :].bitcast(F32), ALU.subtract).then_inc(s_rlo, 1)
                for i in range(TT):
                    v.wait_ge(s_proj, b * (QK + TT) + (QK + i + 1))
                    v.tensor_tensor(vf[:, i % 2, :], banks[i % 2][:, :], v_bias[:, :], ALU.add).then_inc(s_vf, 1)
                    v.wait_ge(s_vhi, b * TT + (i + 1))
                    v.tensor_tensor(val[1][:, i, :], vf[:, i % 2, :], val[0][:, i, :].bitcast(F32), ALU.subtract).then_inc(s_vlo, 1)

                def take(h):
                    r, m = DH0 * (h % 4), h // 4
                    v.wait_ge(core.valued, b * H0 + (h + 2))
                    v.tensor_tensor(xb[r:r + DH0, m, :], xb[r:r + DH0, m, :], core.o_bank[r:r + DH0, :], ALU.add)\
                        .then_inc(core.taken, 1)

                def low(h, i):
                    core.dve_low(v, b * H0 + h, i)

                dve_pipeline(core, v, b * H0, H0, low, take, identity)


def dve_pipeline(core, v, first, heads, low, take, identity, fill=lambda slot: None):
    for u in range(heads + 2):
        if u < heads:
            core.dve_peak(v, first + u, 0)
            core.dve_peak(v, first + u, 1)
        fill((u, "middle"))
        if u >= 2:
            take(u - 2)
        if u < heads:
            core.dve_peak(v, first + u, 2)
            core.dve_peak(v, first + u, 3)
        for i in range(TT):
            if 0 <= u - 1 < heads:
                low(u - 1, i)
        if u < heads:
            core.dve_scale(v, first + u, identity[:, :])
        fill((u, "end"))


ADA = 6 * D // P
SHIFT1, SCALE1, GATE1, SHIFT2, SCALE2, GATE2 = (C * i for i in range(6))
LN_EPS = 1e-6


def row_of(dram, b):
    return dram[:, :, bass.ds(b, 1), :].rearrange("p c o t -> p c (o t)")


def ada_phase(nc, io, cond_dram, ada_dram):
    with ExitStack() as ctx:
        def sb(n, s, d=F32): return ctx.enter_context(nc.sbuf_tensor(n, s, d))
        def sem(n): return ctx.enter_context(nc.semaphore(n))
        QUARTERS = 4
        w = [sb(f"ada_w{i}", [P, C, 6 * D // QUARTERS]) for i in range(QUARTERS)]
        cond = sb("ada_cond", [P, C, B])
        bias = sb("ada_bias", [P, ADA])
        ada = sb("ada", [P, ADA, B])
        bank = ctx.enter_context(nc.psum_tensor("ada_bank", [P, 512], F32))
        s_w = [sem(f"a_w{i}") for i in range(QUARTERS)]
        s_small, s_mm, s_add, s_out = sem("a_small"), sem("a_mm"), sem("a_add"), sem("a_out")
        block = ctx.enter_context(nc.Block())
        w_view = io["L0_cond2_ada_w"].rearrange("(c p) n -> p c n", p=P)

        @block.sync
        def _(sp):
            sp.dma_start(cond[:, :, :], cond_dram).then_inc(s_small, 16)
            for i in range(QUARTERS):
                sp.dma_start(w[i][:, :, :], w_view[:, :, i * 768:(i + 1) * 768]).then_inc(s_w[i], 16)
            sp.wait_ge(s_add, 1)
            sp.dma_start(ada_dram, ada[:, :, :]).then_inc(s_out, 16)
            sp.wait_ge(s_out, 16)

        @block.scalar
        def _(act):
            with nc.allow_non_contiguous_dma(reason="the bias, once"):
                act.dma_start(bias[:, :], io["L0_cond2_ada_b"].rearrange("(m p) -> p m", p=P)).then_inc(s_small, 16)

        @block.tensor
        def _(pe):
            pe.wait_ge(s_small, 32)
            per = ADA // QUARTERS
            for m in range(ADA):
                if m % per == 0:
                    pe.wait_ge(s_w[m // per], 16)
                for k in range(C):
                    last = pe.matmul(bank[:, m * B:(m + 1) * B], w[m // per][:, k, (m % per) * P:(m % per + 1) * P], cond[:, k, :],
                                     start=(m == 0 and k == 0), stop=(m == ADA - 1 and k == C - 1), skip_group_check=True)
            last.then_inc(s_mm, 1)

        @block.vector
        def _(v):
            v.wait_ge(s_mm, 1)
            for b in range(B):
                last = v.tensor_tensor(ada[:, :, b], bank[:, 0:ADA * B].rearrange("p (m b) -> p m b", b=B)[:, :, b], bias[:, :], ALU.add)
            last.then_inc(s_add, 1)


def norm_phase(nc, io, tag, x_dram, ada_dram, shift, scale, gate, bias_name, parts_dram, carried_dram):
    with ExitStack() as ctx:
        def sb(n, s, d=F32): return ctx.enter_context(nc.sbuf_tensor(tag + n, s, d))
        def sem(n): return ctx.enter_context(nc.semaphore(tag + n))
        X = 3
        x = sb("x", [P, X, C, T])
        x_p = [sb(f"x{p}", [P, C, T], F32R) for p in PARTS]
        sq = sb("sq", [P, C, T])
        sq_p = [sb(f"sq{p}", [P, C, T], F32R) for p in PARTS]
        centred = sb("centred", [P, 2, C, T])
        out = sb("out", [P, C, T])
        out_p = [sb(f"out{p}", [P, 2, C, T], F32R) for p in PARTS]
        carried = sb("carried", [P, 2, C, T])
        ada = sb("ada", [P, ADA, B])
        one_plus = sb("one_plus", [P, C, B])
        bias = sb("bias", [P, C])
        gated = sb("gated", [P, C, B])
        mean_f, mean_w = sb("mean_f", [P, P]), sb("mean_w", [P, P], F32R)
        eps = sb("eps", [P, 1])
        dev, inv, var, t1, t2, rstd = [sb(n, [P, T]) for n in ("dev", "inv", "var", "t1", "t2", "rstd")]
        mean_bank, var_bank = [[ctx.enter_context(nc.psum_tensor(f"{tag}{n}{i}", [P, 512], F32)) for i in range(2)] for n in ("mean", "var")]
        s_x = [sem(f"s_x{i}") for i in range(X)]
        s_small, s_pre, s_own = sem("s_small"), sem("s_pre"), sem("s_own")
        s_xhi, s_xlo = sem("s_xhi"), sem("s_xlo")
        s_mean = sem("s_mean")
        s_c = sem("s_c")
        s_sq = sem("s_sq")
        s_qhi, s_qlo = sem("s_qhi"), sem("s_qlo")
        s_var = sem("s_var")
        s_dev = sem("s_dev")
        s_scaled = sem("s_scaled")
        s_shifted = sem("s_shifted")
        s_ohi, s_olo = sem("s_ohi"), sem("s_olo")
        s_car = sem("s_car")
        s_out = [sem("s_out0"), sem("s_out1")]
        block = ctx.enter_context(nc.Block())

        @block.sync
        def _(sp):
            for b in range(B):
                if b >= X:
                    sp.wait_ge(s_c, b - X + 1)
                    sp.wait_ge(s_car, b - X + 1)
                    sp.wait_ge(s_xlo, b - X + 1)
                sp.dma_start(x[:, b % X], row_of(x_dram, b)).then_inc(s_x[b % X], 16)
            for b in range(B):
                sp.wait_ge(s_olo, b + 1)
                sp.wait_ge(s_car, b + 1)
                for p in PARTS:
                    sp.dma_start(row_of(parts_dram[p], b), out_p[p][:, b % 2].bitcast(F32)).then_inc(s_out[b % 2], 16)
                sp.dma_start(row_of(carried_dram, b), carried[:, b % 2]).then_inc(s_out[b % 2], 16)
            for i in range(2):
                sp.wait_ge(s_out[i], 48 * 2)

        @block.scalar
        def _(act):
            act.dma_start(ada[:, :, :], ada_dram).then_inc(s_small, 16)
            with nc.allow_non_contiguous_dma(reason="512 bias values, once"):
                act.dma_start(bias[:, :], io[bias_name].rearrange("(c p) -> p c", p=P)).then_inc(s_small, 16)
            act.wait_ge(s_pre, 1)

            def parts_of_x(b):
                act.wait_ge(s_x[b % X], 16 * (b // X + 1))
                if b >= 1:
                    act.wait_ge(s_mean, b)
                act.activation(x_p[0][:, :, :], x[:, b % X], ACT.Copy).then_inc(s_xhi, 1)

            def square(b):
                act.wait_ge(s_c, b + 1)
                if b >= 1:
                    act.wait_ge(s_qlo, b)
                act.activation(sq[:, :, :], centred[:, b % 2], ACT.Square).then_inc(s_sq, 1)
                act.wait_ge(s_sq, b + 1)
                if b >= 1:
                    act.wait_ge(s_var, b)
                act.activation(sq_p[0][:, :, :], sq[:, :, :], ACT.Copy).then_inc(s_qhi, 1)

            def root(b):
                act.wait_ge(s_var, b + 1)
                if b >= 1:
                    act.wait_ge(s_scaled, b)
                act.activation(dev[:, :], var_bank[b % 2][:, :], ACT.Sqrt, bias=eps[:, :]).then_inc(s_dev, 1)

            def finish(b):
                act.wait_ge(s_scaled, b + 1)
                if b >= 1:
                    act.wait_ge(s_olo, b)
                for c in range(C):
                    last = act.activation(out[:, c, :], centred[:, b % 2, c, :], ACT.Identity, bias=ada[:, shift + c, b:b + 1])
                last.then_inc(s_shifted, 1)
                act.wait_ge(s_shifted, b + 1)
                if b >= 2:
                    act.wait_ge(s_out[b % 2], 48 * (b // 2))
                act.activation(out_p[0][:, b % 2], out[:, :, :], ACT.Copy).then_inc(s_ohi, 1)

            for step in range(B + 2):
                if step >= 2:
                    root(step - 2)
                if step < B:
                    parts_of_x(step)
                if 1 <= step <= B:
                    square(step - 1)
                if step >= 2:
                    finish(step - 2)

        @block.tensor
        def _(pe):
            pe.wait_ge(s_pre, 2)

            def average(bank, parts):
                n = 0
                for k in range(C):
                    for p in PARTS:
                        last = pe.matmul(bank[:, :], mean_w[:, :], parts[p][:, k, :], start=(n == 0), stop=(n == 2 * C - 1))
                        n += 1
                return last

            for step in range(B + 1):
                if step < B:
                    pe.wait_ge(s_xlo, step + 1)
                    if step >= 2:
                        pe.wait_ge(s_c, step - 1)
                    average(mean_bank[step % 2], x_p).then_inc(s_mean, 1)
                if step >= 1:
                    b = step - 1
                    pe.wait_ge(s_qlo, b + 1)
                    if b >= 2:
                        pe.wait_ge(s_scaled, b - 1)
                    average(var_bank[b % 2], sq_p).then_inc(s_var, 1)

        @block.gpsimd
        def _(g):
            for step in range(B + 1):
                if step < B:
                    g.wait_ge(s_xhi, step + 1)
                    g.tensor_tensor(x_p[1][:, :, :], x[:, step % X], x_p[0][:, :, :].bitcast(F32), ALU.subtract).then_inc(s_xlo, 1)
                if step >= 1:
                    g.wait_ge(s_qhi, step)
                    g.tensor_tensor(sq_p[1][:, :, :], sq[:, :, :], sq_p[0][:, :, :].bitcast(F32), ALU.subtract).then_inc(s_qlo, 1)

        @block.vector
        def _(v):
            v.memset(mean_f[:, :], 1.0 / D).then_inc(s_own, 1)
            v.memset(eps[:, :], LN_EPS).then_inc(s_pre, 1)
            v.wait_ge(s_own, 1)
            v.tensor_copy(mean_w[:, :], mean_f[:, :]).then_inc(s_pre, 1)
            v.wait_ge(s_small, 32)
            v.tensor_scalar(one_plus[:, :, :], ada[:, scale:scale + C, :], 1.0, None, ALU.add).then_inc(s_own, 1)
            for b in range(B):
                last = v.tensor_tensor(gated[:, :, b], ada[:, gate:gate + C, b], bias[:, :], ALU.mult)
            last.then_inc(s_own, 1)
            n = 3
            v.wait_ge(s_own, n)

            def own(ins):
                nonlocal n
                ins.then_inc(s_own, 1)
                n += 1
                v.wait_ge(s_own, n)

            def centre(b):
                v.wait_ge(s_mean, b + 1)
                if b >= 2:
                    v.wait_ge(s_shifted, b - 1)
                for c in range(C):
                    last = v.tensor_tensor(centred[:, b % 2, c, :], x[:, b % X, c, :], mean_bank[b % 2][:, :], ALU.subtract)
                last.then_inc(s_c, 1)

            def normalise(b):
                v.wait_ge(s_dev, b + 1)
                v.tensor_scalar(var[:, :], var_bank[b % 2][:, :], LN_EPS, None, ALU.add)
                own(v.reciprocal(inv[:, :], dev[:, :]))
                own(v.tensor_tensor(t1[:, :], inv[:, :], inv[:, :], ALU.mult))
                own(v.scalar_tensor_tensor(out=t2[:, :], in0=t1[:, :], scalar=-0.5, in1=var[:, :], op0=ALU.mult, op1=ALU.mult))
                own(v.scalar_tensor_tensor(out=rstd[:, :], in0=t2[:, :], scalar=1.5, in1=inv[:, :], op0=ALU.add, op1=ALU.mult))
                v.wait_ge(s_sq, b + 1)
                for c in range(C):
                    last = v.scalar_tensor_tensor(out=centred[:, b % 2, c, :], in0=centred[:, b % 2, c, :], scalar=one_plus[:, c, b:b + 1],
                                                  in1=rstd[:, :], op0=ALU.mult, op1=ALU.mult)
                last.then_inc(s_scaled, 1)

            def carry(b):
                v.wait_ge(s_x[b % X], 16 * (b // X + 1))
                if b >= 2:
                    v.wait_ge(s_out[b % 2], 48 * (b // 2))
                for c in range(C):
                    last = v.tensor_scalar(carried[:, b % 2, c, :], x[:, b % X, c, :], gated[:, c, b:b + 1], None, ALU.add)
                last.then_inc(s_car, 1)

            def low_part(b):
                v.wait_ge(s_ohi, b + 1)
                v.tensor_tensor(out_p[1][:, b % 2], out[:, :, :], out_p[0][:, b % 2].bitcast(F32), ALU.subtract).then_inc(s_olo, 1)

            carry(0)
            for step in range(1, B + 2):
                if step <= B:
                    centre(step - 1)
                if step >= 2:
                    normalise(step - 2)
                if step >= 2:
                    low_part(step - 2)
                if step < B:
                    carry(step)


H1, DH1 = 16, 128
GROUP = 4
GROUPS = H1 // GROUP
INNER = H1 * DH1
V_, Q_, K_, O_ = range(4)
WEIGHTS = (O_, Q_, K_, V_)
FIRST = ((Q_, 0), (K_, 0), (Q_, 1), (K_, 1))
FILLS = {(0, "middle"): ((V_, 0),), (0, "end"): ((V_, 1), (Q_, 2), (K_, 2)), (1, "middle"): ((V_, 2),), (1, "end"): ((V_, 3), (Q_, 3)), (2, "middle"): ((K_, 3),),
         (3, "end"): (FIRST[0],), (4, "end"): (FIRST[1], FIRST[2]), (5, "end"): (FIRST[3],)}
ORDER = [tile for fill in FILLS.values() for tile in fill]
OWN = len(ORDER) - len(FIRST)


def attention_phase(nc, io, parts_dram, ada_dram, carried_dram):
    with ExitStack() as ctx:
        def sb(n, s, d=F32): return ctx.enter_context(nc.sbuf_tensor("t_" + n, s, d))
        def sem(n): return ctx.enter_context(nc.semaphore("t_" + n))
        core = Attention(nc, ctx, GROUP, float(DH1) ** -0.5, False, (0, 1, 2, 0))
        banks = [ctx.enter_context(nc.psum_tensor(f"t_bank{i}", [P, 512], F32)) for i in range(2)]
        identity = sb("ident", [P, P])
        x_p = [sb(f"x{p}", [P, C, T], F32R) for p in PARTS]
        raw = sb("raw", [P, 2, C, 512])
        weight = [[sb(f"w{i}{p}", [P, C, 512], F32R) for p in PARTS] for i in range(4)]
        q_p = [sb(f"q{p}", [P, GROUP, T], F32R) for p in PARTS]
        k_p = [sb(f"k{p}", [P, GROUP, T], F32R) for p in PARTS]
        val = [sb(f"v{p}", [P, TT, GROUP * DH1], F32R) for p in PARTS]
        att = [sb(f"a{p}", [P, GROUP, T], F32R) for p in PARTS]
        carried = sb("carried", [P, C, T])
        ada = sb("ada", [P, ADA, B])
        bias = sb("bias", [P, 3, H1])
        bias_now = sb("bias_now", [P, 3, GROUP])
        bias_next = sb("bias_next", [P, 2, 2])
        gate_now = sb("gate_now", [P, C])
        s_small = sem("small")
        s_raw = [sem("raw0"), sem("raw1")]
        s_whi = sem("whi")
        s_wlo = sem("wlo")
        s_x = sem("x")
        s_now = sem("now")
        s_proj = sem("proj")
        s_uhi = sem("uhi")
        s_ulo = sem("ulo")
        s_ahi = sem("ahi")
        s_car = sem("car")
        s_o = sem("o")
        s_added = sem("added")
        s_turn = sem("turn")
        s_turn_g = sem("turn_g")
        s_turn_a = sem("turn_a")
        s_back = sem("back")
        block = ctx.enter_context(nc.Block())
        N = B * GROUPS
        TILES = len(ORDER)
        HEAD = len(FIRST)
        qkv_w = io["L0_cond2_qkv_w"].rearrange("(c p) n -> p c n", p=P)
        out_w = io["L0_cond2_out_w"].rearrange("(h p) n -> p h n", p=P)

        WEIGHT_SLOTS = [(0, "end"), (2, "middle"), (2, "end"), (3, "end")]

        def place(i, group):
            return group * GROUP if i == O_ else group * 512 + {Q_: 0, K_: 1, V_: 2}[i] * INNER

        def source(i, at):
            return out_w[:, bass.ds(at, GROUP), :] if i == O_ else qkv_w[:, :, bass.ds(at, 512)]

        @block.sync
        def _(sp):
            for n, i in enumerate((Q_, K_)):
                sp.dma_start(raw[:, n % 2], source(i, place(i, 0))).then_inc(s_raw[n % 2], 16)
            sp.wait_ge(s_wlo, 3)
            sp.dma_start(raw[:, 0], source(V_, place(V_, 0))).then_inc(s_raw[0], 16)
            with sp.Fori(0, N) as it:
                following = (it + 1) % N
                at = {i: sp.snap(place(i, (it if i == O_ else following) % GROUPS)) for i in WEIGHTS}
                for j, i in enumerate(WEIGHTS):
                    sp.wait_ge(s_wlo, it * 4 + (3 + j + 1))
                    sp.sem_inc(s_turn, 1)
                    sp.dma_start(raw[:, (3 + j) % 2], source(i, at[i])).then_inc(s_raw[(3 + j) % 2], 16)
            sp.wait_ge(s_back, 16 * N)

        @block.gpsimd
        def _(g):
            g.sem_inc(s_wlo, 2)
            g.dma_start(identity[:, :], io["const_identity"]).then_inc(s_small, 16)
            g.dma_start(ada[:, :, :], ada_dram).then_inc(s_small, 16)
            with nc.allow_non_contiguous_dma(reason="6144 bias values, once"):
                g.dma_start(bias[:, :, :], io["L0_cond2_qkv_b"].rearrange("(s m p) -> p s m", s=3, p=P)).then_inc(s_small, 16)

            for n, i in enumerate((Q_, K_, V_)):
                g.wait_ge(s_whi, n + 1)
                g.tensor_tensor(weight[i][1][:, :, :], raw[:, n % 2], weight[i][0][:, :, :].bitcast(F32), ALU.subtract).then_inc(s_wlo, 1)
            g.dma_start(carried[:, :, :], row_of(carried_dram, 0)).then_inc(s_car, 16)
            with g.Fori(0, N) as it:
                row, next_row = g.snap(it // GROUPS), g.snap(((it + 1) % N) // GROUPS)
                for j, i in enumerate(WEIGHTS):
                    g.wait_ge(s_whi, it * 4 + (3 + j + 1))
                    g.tensor_tensor(weight[i][1][:, :, :], raw[:, (3 + j) % 2], weight[i][0][:, :, :].bitcast(F32), ALU.subtract).then_inc(s_wlo, 1)
                g.wait_ge(s_added, it * C + (C + 2))
                g.sem_inc(s_turn_g, 1)
                g.dma_start(row_of(carried_dram, row), carried[:, :, :]).then_inc(s_back, 16)
                g.wait_ge(s_back, 16 * it + 16)
                g.sem_inc(s_turn_g, 1)
                g.dma_start(carried[:, :, :], row_of(carried_dram, next_row)).then_inc(s_car, 16)
            g.wait_ge(s_car, 16 * N + 16)

        def weight_high(act, it, j):
            i = WEIGHTS[j]
            which = (3 + j) % 2
            before = 2 if which == 0 else 1
            act.wait_ge(s_raw[which], it * 32 + 16 * (before + j // 2 + 1))
            if i == O_:
                act.wait_ge(s_o, it * C + C)
            else:
                act.wait_ge(s_proj, it * TILES + (HEAD + OWN))
            act.activation(weight[i][0][:, :, :], raw[:, which], ACT.Copy).then_inc(s_whi, 1)

        @block.scalar
        def _(act):
            core.start_act(act)

            def load_row(row):
                for p in PARTS:
                    act.dma_start(x_p[p][:, :, :].bitcast(F32), row_of(parts_dram[p], row)).then_inc(s_x, 16)

            load_row(0)
            for n, i in enumerate((Q_, K_, V_)):
                act.wait_ge(s_raw[n % 2], 16 * (n // 2 + 1))
                act.activation(weight[i][0][:, :, :], raw[:, n % 2], ACT.Copy).then_inc(s_whi, 1)

            def high_part(place, n, w, h, bias_of):
                act.wait_ge(s_proj, place + (n + 1))
                if w == V_:
                    act.activation(val[0][:, h, :], banks[n % 2][:, :], ACT.Copy).then_inc(s_uhi, 1)
                else:
                    act.activation((q_p if w == Q_ else k_p)[0][:, h, :], banks[n % 2][:, :], ACT.Identity,
                                   bias=bias_of(w, h)).then_inc(s_uhi, 1)

            act.wait_ge(s_small, 48)
            for n, (w, h) in enumerate(FIRST):
                high_part(0, n, w, h, lambda w, h: bias[:, w - Q_, h:h + 1])
            with act.Fori(0, N) as it:
                next_row = act.snap(((it + 1) % N) // GROUPS)

                def fill(slot):
                    for w, h in FILLS.get(slot, ()):
                        n = ORDER.index((w, h))
                        if n == 1:
                            act.wait_ge(s_now, it + 1)
                        high_part(it * TILES + HEAD, n, w, h, lambda w, h: (bias_now if n < OWN else bias_next)[:, w - Q_, h:h + 1])
                    if slot == (2, "middle"):
                        act.wait_ge(s_proj, it * TILES + (HEAD + OWN))
                        act.sem_inc(s_turn_a, 1)
                        load_row(next_row)
                    if slot in WEIGHT_SLOTS:
                        weight_high(act, it, WEIGHT_SLOTS.index(slot))

                def take(h):
                    act.wait_ge(core.valued, it * GROUP + (h + 2))
                    act.activation(att[0][:, h, :], core.o_bank[:, :], ACT.Identity, bias=bias_now[:, 2, h:h + 1]).then_inc(s_ahi, 1)

                pipeline(GROUP, lambda h, i: core.act_exp(act, it * GROUP + h, i, h % 2),
                         lambda h, i: core.act_high(act, it * GROUP + h, i), take, fill)

        @block.tensor
        def _(pe):
            core.start_pe(pe)
            pe.sem_inc(s_o, C)
            pe.wait_ge(s_small, 48)

            def project(place, n, w, h):
                pe.wait_ge(s_ulo, place + (n + 1))
                if w == V_:
                    j = 0
                    for k in range(C):
                        for a, c in PRODUCTS:
                            last = pe.matmul(banks[n % 2][:, :], x_p[a][:, k, h * P:(h + 1) * P], weight[V_][c][:, k, :],
                                             start=(j == 0), stop=(j == 3 * C - 1))
                            j += 1
                else:
                    last = product(pe, banks[n % 2][:, :], lambda a, k: weight[w][a][:, k, h * P:(h + 1) * P], lambda a, k: x_p[a][:, k, :], C)
                last.then_inc(s_proj, 1)

            pe.wait_ge(s_x, 32)
            pe.wait_ge(s_wlo, 4)
            for n, (w, h) in enumerate(FIRST):
                project(0, n, w, h)
            with pe.Fori(0, N) as it:
                def fill(slot):
                    for w, h in FILLS.get(slot, ()):
                        n = ORDER.index((w, h))
                        if n < 2:
                            pe.wait_ge(s_added, it * C + (n + 1))
                        if n == 0:
                            pe.wait_ge(s_wlo, it * 4 + 5)
                        if n == OWN:
                            pe.wait_ge(s_x, 32 * it + 64)
                            pe.wait_ge(s_wlo, it * 4 + 7)
                        if n == OWN + 1:
                            pe.wait_ge(s_wlo, it * 4 + 8)
                        project(it * TILES + HEAD, n, w, h)

                def scores(h, i):
                    if i == 0:
                        pe.wait_ge(s_ulo, it * TILES + (HEAD + 2 + (0 if h < 2 else ORDER.index((K_, h)) + 1)))
                    core.pe_scores(pe, it * GROUP + h, i, [q_p[a][:, h, :] for a in PARTS], [k_p[a][:, h, :] for a in PARTS])

                def values(h):
                    if h == 0:
                        pe.wait_ge(s_ulo, it * TILES + (HEAD + 2 + OWN))
                    core.pe_values(pe, it * GROUP + h, lambda a, j: val[a][:, j, h * DH1:(h + 1) * DH1])

                pipeline(GROUP, scores, lambda h, i: core.pe_turn(pe, it * GROUP + h, i, h % 2), values, fill)
                pe.wait_ge(core.taken, it * GROUP + (GROUP + 1))
                pe.wait_ge(s_wlo, it * 4 + 6)
                for m in range(C):
                    if m < 2:
                        pe.wait_ge(s_ulo, it * TILES + (HEAD + TILES + 1 + m))
                    pe.wait_ge(s_added, it * C + (m + 1))
                    last = product(pe, banks[m % 2][:, :], lambda a, k: weight[O_][a][:, k, m * P:(m + 1) * P], lambda a, k: att[a][:, k, :], GROUP)
                    last.then_inc(s_o, 1)

        @block.vector
        def _(v):
            core.start_dve(v)
            v.sem_inc(core.taken, 1)
            v.sem_inc(s_ulo, 2)
            v.sem_inc(s_added, 2)
            v.wait_ge(s_small, 48)

            def low_part(place, n, w, h, bias_of):
                v.wait_ge(s_uhi, place + (n + 1))
                if w == V_:
                    v.tensor_tensor(val[1][:, h, :], banks[n % 2][:, :], val[0][:, h, :].bitcast(F32), ALU.subtract).then_inc(s_ulo, 1)
                else:
                    hi, lo = [(q_p if w == Q_ else k_p)[p][:, h, :] for p in PARTS]
                    v.scalar_tensor_tensor(out=lo, in0=banks[n % 2][:, :], scalar=bias_of(w, h), in1=hi.bitcast(F32),
                                           op0=ALU.add, op1=ALU.subtract).then_inc(s_ulo, 1)

            for n, (w, h) in enumerate(FIRST):
                low_part(0, n, w, h, lambda w, h: bias[:, w - Q_, h:h + 1])
            with v.Fori(0, N) as it:
                v.wait_ge(core.valued, it * GROUP + 1)
                v.wait_ge(s_ulo, it * TILES + (HEAD + 2))
                v.wait_ge(s_added, it * C + 2)
                v.tensor_copy(gate_now[:, :], ada[:, GATE1:GATE1 + C, bass.ds(it // GROUPS, 1)].rearrange("p c o -> p (c o)"))
                v.tensor_copy(bias_next[:, :, :], bias[:, 0:2, bass.ds(((it + 1) % GROUPS) * GROUP, 2)])
                v.tensor_copy(bias_now[:, :, :], bias[:, :, bass.ds((it % GROUPS) * GROUP, GROUP)]).then_inc(s_now, 1)

                def fill(slot):
                    for w, h in FILLS.get(slot, ()):
                        n = ORDER.index((w, h))
                        if n == 1:
                            v.wait_ge(s_now, it + 1)
                        low_part(it * TILES + HEAD, n, w, h, lambda w, h: (bias_now if n < OWN else bias_next)[:, w - Q_, h:h + 1])

                def take(h):
                    v.wait_ge(s_ahi, it * GROUP + (h + 1))
                    v.scalar_tensor_tensor(out=att[1][:, h, :], in0=core.o_bank[:, :], scalar=bias_now[:, 2, h:h + 1],
                                           in1=att[0][:, h, :].bitcast(F32), op0=ALU.add, op1=ALU.subtract).then_inc(core.taken, 1)

                dve_pipeline(core, v, it * GROUP, GROUP, lambda h, i: core.dve_low(v, it * GROUP + h, i), take, identity, fill)
                v.wait_ge(s_car, 16 * it + 16)
                for m in range(C):
                    v.wait_ge(s_o, it * C + (C + m + 1))
                    v.scalar_tensor_tensor(out=carried[:, m, :], in0=banks[m % 2][:, :], scalar=gate_now[:, m:m + 1],
                                           in1=carried[:, m, :], op0=ALU.mult, op1=ALU.add).then_inc(s_added, 1)


HIDDEN = 4 * D
HT = HIDDEN // P


def ffn_phase(nc, io, sign, parts_dram, ada_dram, base_dram, result):
    with ExitStack() as ctx:
        tag = "b_" if sign else "g_"
        def sb(n, s, d=F32): return ctx.enter_context(nc.sbuf_tensor(tag + n, s, d))
        def sem(n): return ctx.enter_context(nc.semaphore(tag + n))
        WP = (0,) if sign else PARTS
        CHUNK = 4
        RAW = 4
        raw = sb("raw", [P, RAW, CHUNK, 512])
        w1 = [sb(f"w1{p}", [P, C, HIDDEN], F32R) for p in WP]
        w2 = [sb(f"w2{p}", [P, HT, D], F32R) for p in WP]
        x_p = [sb(f"x{p}", [P, C, T], F32R) for p in PARTS]
        h = sb("h", [P, 2, T])
        h_p = [sb(f"h{p}", [P, 2, T], F32R) for p in PARTS]
        base = sb("base", [P, C, T])
        per_hidden = sb("per_hidden", [P, HT])
        identity = sb("ident", [P, P])
        acc = [ctx.enter_context(nc.psum_tensor(f"{tag}acc{i}", [P, 512], F32)) for i in range(C)]
        hb = [ctx.enter_context(nc.psum_tensor(f"{tag}hb{i}", [P, 512], F32)) for i in range(2)]
        s_small = sem("small")
        s_raw = [sem(f"raw{i}") for i in range(RAW)]
        s_tr, s_whi, s_wlo = sem("tr"), sem("whi"), sem("wlo")
        s_x, s_xp, s_base = sem("x"), sem("xp"), sem("base")
        s_h = sem("h")
        s_act = sem("act")
        s_hhi = sem("hhi")
        s_hlo = sem("hlo")
        s_used = sem("used")
        s_done = sem("done")
        s_out = sem("out")
        s_own = sem("own")
        gate = sb("gate", [P, C, B])
        gate_now = sb("gate_now", [P, C])
        if sign:
            x32 = sb("x32", [P, C, T])
            final = sb("final", [P, C, T])
            tokens = sb("tokens", [P, 2, D])
            down_scale, output_scale = sb("down_scale", [P, C]), sb("output_scale", [P, 1])
            s_tt, s_tok, s_sent = sem("tt"), sem("tok"), [sem("sent0"), sem("sent1")]
            tb = [ctx.enter_context(nc.psum_tensor(f"{tag}tb{i}", [P, 512], F32)) for i in range(2)]
            loads = [io["L0_ffn_up_weight"][512 * i:512 * (i + 1), :].rearrange("(c p) n -> p c n", p=P) for i in range(4)]
            loads += [io["L0_ffn_down_weight"].rearrange("(c p) n -> p c n", p=P)[:, :, 512 * i:512 * (i + 1)] for i in range(4)]
        else:
            ada = sb("ada", [P, ADA, B])
            loads = [io["L0_cond2_ffn_w1"].rearrange("(c p) n -> p c n", p=P)[:, :, 512 * i:512 * (i + 1)] for i in range(4)]
            loads += [io["L0_cond2_ffn_w2"][512 * i:512 * (i + 1), :].rearrange("(c p) n -> p c n", p=P) for i in range(4)]
        NL = len(loads)
        block = ctx.enter_context(nc.Block())

        def part(p, n):
            return w1[p][:, :, 512 * n:512 * (n + 1)] if n < 4 else w2[p][:, 4 * (n - 4):4 * (n - 3), :]

        @block.sync
        def _(sp):
            for n in range(NL):
                if n >= RAW:
                    done = n - RAW + 1
                    sp.wait_ge(s_tr if sign else s_wlo, 4 * done if sign else done)
                sp.dma_start(raw[:, n % RAW], loads[n]).then_inc(s_raw[n % RAW], 16)
            with sp.Fori(0, B) as b:
                if sign:
                    sp.wait_ge(s_done, b * C + C)
                else:
                    sp.wait_ge(s_out, 16 * b + 16)
                sp.dma_start(base[:, :, :], row_of(base_dram, b)).then_inc(s_base, 16)
                if not sign:
                    sp.wait_ge(s_done, b * C + (2 * C))
                    sp.dma_start(row_of(result, b), base[:, :, :]).then_inc(s_out, 16)
                else:
                    for i in range(TT):
                        sp.wait_ge(s_tok, b * TT + (i + 3))
                        sp.dma_start(result[bass.ds(b, 1), i * P:(i + 1) * P, :].rearrange("o p n -> (o p) n"), tokens[:, i % 2, :]).then_inc(s_sent[i % 2], 16)
            if sign:
                for i in range(2):
                    sp.wait_ge(s_sent[i], 16 * (B * TT // 2) + 16)
            else:
                sp.wait_ge(s_out, 16 * B + 16)

        @block.gpsimd
        def _(g):
            g.dma_start(identity[:, :], io["const_identity"]).then_inc(s_small, 16)
            with nc.allow_non_contiguous_dma(reason="2048 values, once"):
                g.dma_start(per_hidden[:, :], io["L0_ffn_up_scale" if sign else "L0_cond2_ffn_b1"].rearrange("(m p) -> p m", p=P)).then_inc(s_small, 16)
                if sign:
                    g.dma_start(down_scale[:, :], io["L0_ffn_down_scale"].rearrange("(c p) -> p c", p=P)).then_inc(s_small, 16)
                    g.dma_start(output_scale[:, :], io["L0_ffn_output_scale"].partition_broadcast(P)).then_inc(s_small, 16)
                else:
                    g.dma_start(ada[:, :, :], ada_dram).then_inc(s_small, 32)
            with g.Fori(0, B) as b:
                g.wait_ge(s_act, b * HT + 2)
                if sign:
                    g.dma_start(x32[:, :, :], row_of(parts_dram[0], b)).then_inc(s_x, 32)
                else:
                    for p in PARTS:
                        g.dma_start(x_p[p][:, :, :].bitcast(F32), row_of(parts_dram[p], b)).then_inc(s_x, 16)

        @block.tensor
        def _(pe):
            pe.sem_inc(s_used, 2)
            pe.wait_ge(s_small, 64)
            if sign:
                for n in range(NL):
                    pe.wait_ge(s_raw[n % RAW], 16 * (n // RAW + 1))
                    for r in range(4):
                        q = 4 * n + r
                        if q >= 2:
                            pe.wait_ge(s_whi, q - 1)
                        for c in range(4):
                            last = pe.matmul(tb[q % 2][:, c * P:(c + 1) * P], raw[:, n % RAW, c, r * P:(r + 1) * P], identity[:, :],
                                             start=(c == 0), stop=(c == 3), skip_group_check=True)
                        last.then_inc(s_tr, 1)
                pe.wait_ge(s_whi, 4 * NL)
            else:
                pe.wait_ge(s_wlo, NL)
            with pe.Fori(0, B) as b:
                if sign:
                    pe.wait_ge(s_xp, 2 * b + 2)
                else:
                    pe.wait_ge(s_x, 32 * b + 32)

                def hidden(j):
                    pe.wait_ge(s_act, b * HT + (j + 1))
                    n, total = 0, C * (2 if sign else 3)
                    for k in range(C):
                        for a, c in (((0, 0), (0, 1)) if sign else PRODUCTS):
                            last = pe.matmul(hb[j % 2][:, :], w1[a][:, k, j * P:(j + 1) * P], x_p[c][:, k, :], start=(n == 0), stop=(n == total - 1))
                            n += 1
                    last.then_inc(s_h, 1)

                def output(j):
                    if j == 0:
                        pe.wait_ge(s_done, b * C + C)
                    pe.wait_ge(s_hlo, b * HT + (j + 1))
                    pairs = ((0, 0), (0, 1)) if sign else PRODUCTS
                    for m in range(C):
                        for i, (a, c) in enumerate(pairs):
                            last = pe.matmul(acc[m][:, :], w2[a][:, j, m * P:(m + 1) * P], h_p[c][:, j % 2, :],
                                             start=(j == 0 and i == 0), stop=(j == HT - 1 and i == len(pairs) - 1))
                    last.then_inc(s_used, 1)

                hidden(0)
                for j in range(1, HT):
                    hidden(j)
                    output(j - 1)
                output(HT - 1)
                if sign:
                    pe.wait_ge(s_done, b * C + 2 * C)
                    for i in range(TT):
                        pe.wait_ge(s_tok, b * TT + (i + 1))
                        for c in range(C):
                            last = pe.matmul(tb[i % 2][:, c * P:(c + 1) * P], final[:, c, i * P:(i + 1) * P], identity[:, :],
                                             start=(c == 0), stop=(c == C - 1), skip_group_check=True)
                        last.then_inc(s_tt, 1)

        @block.scalar
        def _(act):
            act.sem_inc(s_act, 2)
            if sign:
                for q in range(4 * NL):
                    n, r = q // 4, q % 4
                    act.wait_ge(s_tr, q + 1)
                    dst = w1[0][:, r, 512 * n:512 * (n + 1)] if n < 4 else w2[0][:, 4 * (n - 4) + r, :]
                    act.activation(dst, tb[q % 2][:, :], ACT.Sign).then_inc(s_whi, 1)
            else:
                for n in range(NL):
                    act.wait_ge(s_raw[n % RAW], 16 * (n // RAW + 1))
                    act.activation(part(0, n), raw[:, n % RAW], ACT.Copy).then_inc(s_whi, 1)
            act.wait_ge(s_small, 64)
            with act.Fori(0, B) as b:
                if sign:
                    act.wait_ge(s_x, 32 * b + 32)
                    act.activation(x_p[0][:, :, :], x32[:, :, :], ACT.Copy).then_inc(s_xp, 1)
                for j in range(HT):
                    act.wait_ge(s_h, b * HT + (j + 1))
                    if j >= 2:
                        act.wait_ge(s_hlo, b * HT + (j - 1))
                    if sign:
                        act.activation(h[:, j % 2, :], hb[j % 2][:, :], ACT.Relu, scale=per_hidden[:, j:j + 1]).then_inc(s_act, 1)
                    else:
                        act.activation(h[:, j % 2, :], hb[j % 2][:, :], ACT.Gelu, bias=per_hidden[:, j:j + 1]).then_inc(s_act, 1)
                    act.wait_ge(s_act, b * HT + (j + 3))
                    act.wait_ge(s_used, b * HT + (j + 1))
                    act.activation(h_p[0][:, j % 2, :], h[:, j % 2, :], ACT.Copy).then_inc(s_hhi, 1)

        @block.vector
        def _(v):
            v.sem_inc(s_done, C)
            v.sem_inc(s_out, 16)
            if sign:
                v.sem_inc(s_tok, 2)
                for i in range(2):
                    v.sem_inc(s_sent[i], 16)
            else:
                for n in range(NL):
                    v.wait_ge(s_whi, n + 1)
                    v.tensor_tensor(part(1, n), raw[:, n % RAW], part(0, n).bitcast(F32), ALU.subtract).then_inc(s_wlo, 1)
            v.wait_ge(s_small, 64)
            for b in range(B):
                if sign:
                    last = v.tensor_scalar(gate[:, :, b], down_scale[:, :], output_scale[:, 0:1], None, ALU.mult)
                else:
                    last = v.tensor_copy(gate[:, :, b], ada[:, GATE2:GATE2 + C, b])
            last.then_inc(s_own, 1)
            v.wait_ge(s_own, 1)
            with v.Fori(0, B) as b:
                v.wait_ge(s_done, b * C + C)
                v.tensor_copy(gate_now[:, :], gate[:, :, bass.ds(b, 1)].rearrange("p c o -> p (c o)")).then_inc(s_own, 1)
                if sign:
                    v.wait_ge(s_xp, 2 * b + 1)
                    v.tensor_tensor(x_p[1][:, :, :], x32[:, :, :], x_p[0][:, :, :].bitcast(F32), ALU.subtract).then_inc(s_xp, 1)
                for j in range(HT):
                    v.wait_ge(s_hhi, b * HT + (j + 1))
                    v.tensor_tensor(h_p[1][:, j % 2, :], h[:, j % 2, :], h_p[0][:, j % 2, :].bitcast(F32), ALU.subtract).then_inc(s_hlo, 1)
                v.wait_ge(s_used, b * HT + (HT + 2))
                v.wait_ge(s_base, 16 * b + 16)
                v.wait_ge(s_own, b + 2)
                for m in range(C):
                    v.scalar_tensor_tensor(out=(final if sign else base)[:, m, :], in0=acc[m][:, :], scalar=gate_now[:, m:m + 1],
                                           in1=base[:, m, :], op0=ALU.mult, op1=ALU.add).then_inc(s_done, 1)
                if sign:
                    for i in range(TT):
                        v.wait_ge(s_tt, b * TT + (i + 1))
                        v.wait_ge(s_sent[i % 2], 32 * b + 16 * (i // 2 + 1))
                        v.tensor_copy(tokens[:, i % 2, :], tb[i % 2][:, :]).then_inc(s_tok, 1)


_INS = ['x', 'cond_2048', 'L0_cond_coupling', 'L0_cond_bias', 'L0_attn_Wqkv_w', 'L0_attn_Wqkv_b', 'L0_cond2_ada_w',
        'L0_cond2_ada_b', 'L0_cond2_qkv_w', 'L0_cond2_qkv_b', 'L0_cond2_out_w', 'L0_cond2_out_b', 'L0_cond2_ffn_w1',
        'L0_cond2_ffn_b1', 'L0_cond2_ffn_w2', 'L0_cond2_ffn_b2', 'L0_ffn_up_weight', 'L0_ffn_down_weight',
        'L0_ffn_up_scale', 'L0_ffn_down_scale', 'L0_ffn_output_scale']


def constants():
    half = DH0 // 2
    inv = (np.float32(1.0) / np.float32(10000.0) ** (np.arange(0, DH0, 2, dtype=np.float32) / np.float32(DH0))).astype(np.float32)
    freqs = np.outer(np.arange(T, dtype=np.float32), inv).astype(np.float32)
    lane = np.arange(P) % DH0
    cos = np.cos(freqs).astype(np.float32).T[lane % half]
    sin = np.sin(freqs).astype(np.float32).T[lane % half] * np.where(lane < half, -1.0, 1.0).astype(np.float32)[:, None]
    swap = np.zeros((P, P), np.float32)
    swap[np.arange(P) ^ half, np.arange(P)] = 1.0
    mask = np.where(np.arange(T)[None, :] > np.arange(P)[:, None], NEG_INF, 0.0).astype(np.float32)
    return {"const_identity": np.eye(P, dtype=np.float32), "const_cos": np.ascontiguousarray(cos),
            "const_sin": np.ascontiguousarray(sin), "const_swap": swap, "const_mask": mask}


def program(nc, io, out):
    def dram(name, dt=F32): return nc.dram_tensor(name, (P, C, B, T), dt, kind="Internal").ap()
    x_dram, trace_dram, xa_dram, x2_dram, x3_base, x3_dram = [dram(n) for n in ("x_t", "trace_t", "xa_t", "x2_t", "x3b_t", "x3_t")]
    n1 = [dram(f"n1_{p}") for p in PARTS]
    n2 = [dram(f"n2_{p}") for p in PARTS]
    cond_dram = nc.dram_tensor("cond_t", (P, C, B), F32, kind="Internal").ap()
    ada_dram = nc.dram_tensor("ada_t", (P, ADA, B), F32, kind="Internal").ap()
    scan_phase(nc, io, x_dram, trace_dram, cond_dram)
    causal_phase(nc, io, x_dram, trace_dram, xa_dram)
    ada_phase(nc, io, cond_dram, ada_dram)
    norm_phase(nc, io, "n_", xa_dram, ada_dram, SHIFT1, SCALE1, GATE1, "L0_cond2_out_b", n1, x2_dram)
    attention_phase(nc, io, n1, ada_dram, x2_dram)
    norm_phase(nc, io, "o_", x2_dram, ada_dram, SHIFT2, SCALE2, GATE2, "L0_cond2_ffn_b2", n2, x3_base)
    ffn_phase(nc, io, False, n2, ada_dram, x3_base, x3_dram)
    ffn_phase(nc, io, True, [x3_dram], None, xa_dram, out)


def kernel(**inputs):
    import concourse.bacc as bacc
    from concourse.bass_utils import run_bass_kernel_spmd
    nc = bacc.Bacc("TRN2", target_bir_lowering=False, num_devices=1)
    arrays, io = {}, {}
    host = {name: np.ascontiguousarray(inputs[name]) for name in _INS}
    host.update(constants())
    for name, a in host.items():
        arrays[name + "_dram"] = a
        io[name] = nc.dram_tensor(name + "_dram", a.shape, mybir.dt.from_np(a.dtype), kind="ExternalInput").ap()
    out = nc.dram_tensor("out_dram", (B, T, D), F32, kind="ExternalOutput").ap()
    program(nc, io, out)
    return run_bass_kernel_spmd(nc, [arrays], core_ids=[0]).results[0]["out_dram"]
```
